# Optimizing a Trainium2 kernel written in Bass

```python
import numpy as np
import jax
import jax.numpy as jnp

def _softmax(x, axis=-1):
    return jax.nn.softmax(x, axis=axis)

def _gelu(x):
    return jax.nn.gelu(x, approximate=True)

def _silu(x):
    return jax.nn.silu(x)

def _sigmoid(x):
    return jax.nn.sigmoid(x)

def _layernorm(x, axis=-1, eps=1e-05):
    m = jnp.mean(x, axis=axis, keepdims=True)
    v = jnp.var(x, axis=axis, keepdims=True)
    return (x - m) / jnp.sqrt(v + eps)

def _scatter_add(tgt, idx, src, axis=0):
    return tgt.at[idx].add(src)

def _segment_sum(src, seg, n):
    return jax.ops.segment_sum(src, seg, n)
kernel_name = 'mk_gnn_resnorm_d1_gnn_r8_36cd62'

def setup_inputs(seed: int=0):
    np.random.seed(seed)
    _w = jnp.asarray

    def _rec_inputs():
        import jax
        import jax.numpy as jnp
        _gk = jax.random.key(seed)
        x = -0.000202 + 1 * jax.random.normal(jax.random.fold_in(_gk, 1), (12500, 128), jnp.float32)
        _s = jax.random.randint(jax.random.fold_in(_gk, 2), (100000,), 0, 12500, jnp.int32)
        _d = jax.random.randint(jax.random.fold_in(_gk, 3), (100000,), 0, 12500, jnp.int32)
        _loop = jnp.arange(12500, dtype=jnp.int32)
        src = jnp.concatenate([_s, _d, _loop])
        dst = jnp.concatenate([_d, _s, _loop])
        _o = jnp.argsort(dst, stable=True)
        src = src[_o]
        dst = dst[_o]
        edge_attr_128 = -4.21973e-05 + 0.999841 * jax.random.normal(jax.random.fold_in(_gk, 11), (212500, 128), jnp.float32)
        return (x, src, dst, edge_attr_128)
    x, src, dst, edge_attr_128 = _rec_inputs()

    def _L0_gnn_setup():
        import jax, jax.numpy as jnp
        import numpy as np
        NUM_HEADS = 8
        BN_EPS = 1e-05
        ATTN_EPS = 1e-06
        key = jax.random.key(seed)
        N, E, D = (6250, 75000, 128)
        ks = jax.random.split(key, 7)
        s = 1.0 / np.sqrt(D).astype(np.float32)
        return {'x': jax.random.normal(ks[0], (N, D), jnp.float32), 'edge_attr': jax.random.normal(ks[1], (E, D), jnp.float32), 'WQ': jax.random.normal(ks[2], (D, D), jnp.float32) * s, 'WK': jax.random.normal(ks[3], (D, D), jnp.float32) * s, 'WV': jax.random.normal(ks[4], (D, D), jnp.float32) * s, 'WE': jax.random.normal(ks[5], (D, D), jnp.float32) * s, 'bn_gamma': jnp.ones((D,), jnp.float32), 'bn_beta': jnp.zeros((D,), jnp.float32), 'edge_index': jax.random.randint(ks[6], (2, E), 0, N, dtype=jnp.int32)}
    _L0_gnn_all = _L0_gnn_setup()
    _L0_gnn_in = {k: v for k, v in _L0_gnn_all.items() if k in ('WQ', 'WK', 'WV', 'WE', 'bn_gamma', 'bn_beta')}
    del _L0_gnn_all
    return {'x': x, 'src': src, 'dst': dst, 'edge_attr_128': edge_attr_128, 'L0_gnn_WQ': _L0_gnn_in['WQ'], 'L0_gnn_WK': _L0_gnn_in['WK'], 'L0_gnn_WV': _L0_gnn_in['WV'], 'L0_gnn_WE': _L0_gnn_in['WE'], 'L0_gnn_bn_gamma': _L0_gnn_in['bn_gamma'], 'L0_gnn_bn_beta': _L0_gnn_in['bn_beta']}

def reference(x, src, dst, edge_attr_128, L0_gnn_WQ, L0_gnn_WK, L0_gnn_WV, L0_gnn_WE, L0_gnn_bn_gamma, L0_gnn_bn_beta):
    import jax
    import jax.numpy as jnp

    def _L0_gnn_ref(x, edge_attr, WQ, WK, WV, WE, bn_gamma, bn_beta, edge_index):
        import jax, jax.numpy as jnp
        import numpy as np
        NUM_HEADS = 8
        BN_EPS = 1e-05
        ATTN_EPS = 1e-06
        N, D = x.shape
        H = NUM_HEADS
        dh = D // H
        Q = (x @ WQ).reshape(N, H, dh)
        K = (x @ WK).reshape(N, H, dh)
        V = (x @ WV).reshape(N, H, dh)
        Eh = (edge_attr @ WE).reshape(-1, H, dh)
        src, dst = (edge_index[0], edge_index[1])
        score = K[src] * Q[dst] / jnp.sqrt(jnp.float32(dh)) * Eh
        score = jnp.exp(jnp.clip(score.sum(-1, keepdims=True), -5.0, 5.0))
        msg = V[src] * score
        wV = jax.ops.segment_sum(msg, dst, num_segments=N)
        Z = jax.ops.segment_sum(score, dst, num_segments=N)
        h_attn = (wV / (Z + ATTN_EPS)).reshape(N, D)
        h = x + h_attn
        mean = h.mean(axis=0)
        var = jnp.mean((h - mean) ** 2, axis=0)
        return (h - mean) * jax.lax.rsqrt(var + BN_EPS) * bn_gamma + bn_beta
    edge_index = jnp.stack([src, dst])
    x = _layernorm(x + _L0_gnn_ref(x, edge_attr_128, L0_gnn_WQ, L0_gnn_WK, L0_gnn_WV, L0_gnn_WE, L0_gnn_bn_gamma, L0_gnn_bn_beta, edge_index), axis=-1)
    return x

_drawn_inputs = setup_inputs


def setup_inputs(seed=0):
    import zlib

    import numpy as np

    out = dict(_drawn_inputs(seed))
    spreads = {'L0_gnn_bn_gamma': (1.0, 0.2), 'L0_gnn_bn_beta': (0.0, 0.1)}
    factors = {}
    for name, (base, spread) in spreads.items():
        noise = np.random.default_rng([zlib.crc32(name.encode()), seed]).standard_normal(out[name].shape)
        drawn = base * np.exp(spread * noise) if base else spread * noise
        out[name] = jnp.asarray(drawn.astype(out[name].dtype))
    for name, factor in factors.items():
        out[name] = (out[name] * factor).astype(out[name].dtype)
    return out
```

```python
P = 128
HEADS = 8
TILES = 4
EG = P * TILES
WIN = 64
UNROLL = 4
NB = 512
HALF = 128
BN_EPS = 1e-5
ATTN_EPS = 1e-6
LN_EPS = 1e-5


def build(nc, x, src, dst, edge_attr, wq, wk, wv, we, gamma, beta, out):
    from contextlib import ExitStack

    import concourse.bass as bass
    from concourse import mybir

    F32, I32, BF16 = mybir.dt.float32, mybir.dt.int32, mybir.dt.bfloat16
    ALU = mybir.AluOpType
    ACT = mybir.ActivationFunctionType
    AX = mybir.AxisListType
    ds = bass.ds

    N, D = x.shape
    E = src.shape[0]
    DH = D // HEADS
    KV = 2 * D
    WHOLE = E // EG
    TAIL = E - WHOLE * EG
    NG = WHOLE + 1
    TURNS = NG // UNROLL
    LAST0 = E - EG
    OLD = EG - TAIL
    NPAD = N + WIN
    assert D == P and NG % UNROLL == 0 and 0 < TAIL < EG and OLD % TILES == 0
    ROWTILES = [P] * (WHOLE // P) + [WHOLE % P, 1]
    RT = len(ROWTILES)
    CHUNKS = N // NB
    NLAST = N - NB
    assert CHUNKS % 2 == 0
    CLEAR = 2 * NPAD // CHUNKS
    assert CLEAR * CHUNKS == 2 * NPAD
    HC = 500
    HN = N // HC
    assert HN * HC == N and HN % 2 == 1
    SWEEP = -(-N // (2 * HALF))
    assert SWEEP * 2 * HALF <= NPAD

    with ExitStack() as ctx:
        def sb(name, shape, dt=F32):
            return ctx.enter_context(nc.sbuf_tensor(name, shape, dt))

        def bank(name):
            return ctx.enter_context(nc.psum_tensor(name, [P, 512], F32))

        def sem(name):
            return ctx.enter_context(nc.semaphore(name))

        kv_rows = nc.dram_tensor("kv_rows", (N, KV), F32).ap()
        q_rows = nc.dram_tensor("q_rows", (NPAD, D), F32).ap()
        rel_rows = nc.dram_tensor("rel_rows", (NG, EG), BF16).ap()

        eaT_ps = [bank(f"eaT_ps{b}") for b in range(2)]
        qe_ps = [bank(f"qe_ps{b}") for b in range(2)]
        eh_ps = [bank(f"eh_ps{b}") for b in range(2)]
        agg_ps = [bank(f"agg_ps{b}") for b in range(2)]
        proj_ps = qe_ps + eh_ps

        xT = sb("xT", [P, N])
        acc = sb("acc", [P, 2, NPAD])
        src_t = sb("src_t", [P, NG + UNROLL, TILES])
        rel_t = sb("rel_t", [P, NG, TILES])
        base_i = sb("base_i", [1, NG], I32)
        ident = sb("ident", [P, P])
        ones = sb("ones", [P, 1])
        iota = sb("iota", [P, HALF])
        place_i = sb("place_i", [P, 1], I32)
        minus_p = sb("minus_p", [P, 1])
        w_all = sb("w_all", [P, KV + D])
        we_sb = sb("we_sb", [P, D])
        gam = sb("gam", [P, 1])
        bet = sb("bet", [P, 1])
        eps_attn = sb("eps_attn", [P, 1])
        eps_bn = sb("eps_bn", [P, 1])
        eps_ln = sb("eps_ln", [P, 1])
        one_col = sb("one_col", [P, 1])
        zero_col = sb("zero_col", [P, 1])
        inside = sb("inside", [P, RT])
        inside_all = sb("inside_all", [1, 1])
        stray_i = sb("stray_i", [1, 1], I32)

        acc_flat = acc[:, :, :].rearrange("p a n -> p (a n)")

        def table(k, dt=F32):
            v = acc_flat[:, k * RT * EG:(k + 1) * RT * EG]
            v = v if dt == F32 else v.bitcast(dt)
            return v.rearrange("p (r e) -> p r e", r=RT)

        dst_i, src_i = table(0, I32), table(1, I32)
        dst_f, src_f, rel_f, low_f = table(2), table(3), table(4), table(5)
        assert 7 * RT * EG <= 2 * NPAD
        rel_b = acc_flat[:, 6 * RT * EG:7 * RT * EG].bitcast(BF16)[:, 0:RT * EG].rearrange("p (r e) -> p r e", r=RT)

        ea = sb("ea", [P, UNROLL, TILES, D])
        eaT = sb("eaT", [P, 2, EG])
        relb = sb("relb", [WIN, 2, EG], BF16)
        far = sb("far", [WIN, EG], BF16)
        ohT = sb("ohT", [WIN, 2, EG])
        qwin = sb("qwin", [WIN, 2, D])
        idx = sb("idx", [P, UNROLL, TILES], I32)
        kv = sb("kv", [P, UNROLL, TILES, KV])
        x_in = ea[:, 2:4]
        kv_flat = kv[:, :, :, :].rearrange("p u j d -> p (u j d)")
        proj = kv_flat[:, 0:2 * (NB // P) * (KV + D)].rearrange("p (b j d) -> p b j d", b=2, j=NB // P)

        kq = sb("kq", [P, TILES, D])
        ssum = sb("ssum", [P, TILES * HEADS])
        sclip = sb("sclip", [P, 2, TILES * HEADS])
        score = sb("score", [P, TILES * HEADS, DH])
        onehot = sb("onehot", [P, 2, TILES, WIN])
        iota_i = kq[:, :, :].rearrange("p j d -> p (j d)")[:, 0:HALF].bitcast(I32)
        zeros = onehot[0:WIN, 0].rearrange("p j n -> p (j n)")[:, 0:D]

        bn = sb("bn", [P, 8])
        stats = onehot[:, :, :, :].rearrange("p b j n -> p (b j n)")
        hstat = stats[:, 0:HN * 6].rearrange("p (k s) -> p k s", s=6)
        ystat = stats[:, HN * 6:(HN + 2 * TILES) * 6].rearrange("p (b j s) -> p b j s", b=2, s=6)
        ymv = sb("ymv", [P, 2, TILES, 2])
        ystd = sb("ystd", [P, 2, TILES])
        yrec = sb("yrec", [P, 2, TILES])
        ymr = sb("ymr", [P, 2, TILES])

        consts_made = sem("consts_made")
        consts_cast = sem("consts_cast")
        ident_zero = sem("ident_zero")
        w_landed = sem("w_landed")
        wq_scaled = sem("wq_scaled")
        dst_landed = sem("dst_landed")
        src_landed = sem("src_landed")
        base_landed = sem("base_landed")
        cast_done = sem("cast_done")
        rel_done = sem("rel_done")
        low_done = sem("low_done")
        inside_done = sem("inside_done")
        relb_cast = sem("relb_cast")
        rel_stored = sem("rel_stored")
        tab_turned = sem("tab_turned")
        tab_copied = sem("tab_copied")
        inside_sum = sem("inside_sum")
        stray_step = sem("stray_step")
        stray_known = sem("stray_known")
        acc_clear = sem("acc_clear")
        src_pad = sem("src_pad")
        rel_masked = sem("rel_masked")
        pad_stored = sem("pad_stored")

        x_landed = [sem(f"x_landed{b}") for b in range(2)]
        kv_stored = [sem(f"kv_stored{b}") for b in range(2)]
        q_stored = [sem(f"q_stored{b}") for b in range(2)]
        xT_turned = sem("xT_turned")
        xT_copied = sem("xT_copied")
        xT_kept = sem("xT_kept")
        proj_ready = sem("proj_ready")
        proj_act = sem("proj_act")
        proj_dve = sem("proj_dve")

        ea_landed = [sem(f"ea_landed{u}") for u in range(UNROLL)]
        relb_landed = [sem(f"relb_landed{u}") for u in range(UNROLL)]
        qwin_landed = [sem(f"qwin_landed{u}") for u in range(UNROLL)]
        kv_landed = [sem(f"kv_landed{u}") for u in range(UNROLL)]
        idx_ready = sem("idx_ready")
        gather_begun = sem("gather_begun")
        eaT_ready = sem("eaT_ready")
        eaT_copied = sem("eaT_copied")
        far_done = sem("far_done")
        ohT_ready = sem("ohT_ready")
        qe_ready = sem("qe_ready")
        eh_ready = sem("eh_ready")
        kq_done = sem("kq_done")
        prod_done = sem("prod_done")
        ssum_done = sem("ssum_done")
        clip_done = sem("clip_done")
        exp_done = sem("exp_done")
        onehot_done = sem("onehot_done")
        msg_done = sem("msg_done")
        agg_ready = sem("agg_ready")
        agg_added = sem("agg_added")

        st_ends = idx
        st_q = kv[:, 1, :, 0:D]
        st_onehot = kv[:, 2]
        st_low = sclip[:, 0, 0:TILES]
        st_in = sclip[:, 0, TILES:2 * TILES]
        st_key = sclip[:, 0, 2 * TILES:3 * TILES]
        st_key_hi = sclip[:, 0, 3 * TILES:4 * TILES]
        st_begun = sem("st_begun")
        st_loaded = sem("st_loaded")
        st_gathering = sem("st_gathering")
        st_gathered = sem("st_gathered")
        st_turned = sem("st_turned")
        st_eaT = sem("st_eaT")
        st_eh = sem("st_eh")
        st_step = sem("st_step")
        st_clip = sem("st_clip")
        st_exp = sem("st_exp")
        st_keyed = sem("st_keyed")
        st_onehots = sem("st_onehots")
        st_summed = sem("st_summed")
        st_added = sem("st_added")

        def strays(eng, group_body):
            eng.wait_ge(stray_known, 1)
            count = eng.value_load(stray_i[0:1, 0:1], min_val=0, max_val=E)
            with eng.If(count > 0):
                with eng.Fori(0, NG - 1) as g:
                    group_body(g, False)
                group_body(NG - 1, True)

        z_done = sem("z_done")
        zr_done = sem("zr_done")
        att_done = sem("att_done")
        h_done = sem("h_done")
        hstat_done = sem("hstat_done")
        bn_step = sem("bn_step")
        bn_std = sem("bn_std")
        bn_known = sem("bn_known")
        y1_done = sem("y1_done")
        y_done = sem("y_done")
        yT_ready = sem("yT_ready")
        ystat_done = sem("ystat_done")
        aggr_begun = sem("aggr_begun")
        yaggr_done = sem("yaggr_done")
        ystd_done = sem("ystd_done")
        yrec_done = sem("yrec_done")
        ynorm_known = sem("ynorm_known")
        o_done = sem("o_done")
        out_stored = [sem(f"out_stored{b}") for b in range(2)]

        def group(i, u, k=0):
            t, s = i + (u + k) // UNROLL, (u + k) % UNROLL
            return t, s, t * UNROLL + s

        def rows_of(r):
            return ROWTILES[r]

        def first_row(r):
            return sum(ROWTILES[:r])

        block = ctx.enter_context(nc.Block())

        @block.sync
        def _(sp):
            for ends, table_i, landed in ((dst, dst_i, dst_landed), (src, src_i, src_landed)):
                for r in range(RT):
                    e0 = first_row(r) * EG if r < RT - 1 else LAST0
                    part = ends[e0:e0 + rows_of(r) * EG].rearrange("(g e) -> g e", e=EG)
                    sp.dma_start(table_i[0:rows_of(r), r, :], part).then_inc(landed, 16)
            for k, w in enumerate((wk, wv, wq)):
                sp.dma_start(w_all[:, k * D:(k + 1) * D], w).then_inc(w_landed, 16)
            sp.dma_start(we_sb[:, :], we).then_inc(w_landed, 16)
            sp.dma_start(gam[:, :], gamma.rearrange("(d a) -> d a", a=1)).then_inc(w_landed, 16)
            sp.dma_start(bet[:, :], beta.rearrange("(d a) -> d a", a=1)).then_inc(w_landed, 16)
            with nc.allow_non_contiguous_dma(reason="one word of each group"):
                firsts = dst[0:WHOLE * EG].rearrange("(a g e) -> a g e", a=1, e=EG)[:, :, 0:1]
                sp.dma_start(base_i[0:1, 0:WHOLE].rearrange("a (g b) -> a g b", b=1), firsts).then_inc(base_landed, 16)
                sp.dma_start(base_i[0:1, WHOLE:NG], dst[E - TAIL:E - TAIL + 1].rearrange("(a b) -> a b", a=1)).then_inc(base_landed, 16)

            def load_x(c, b, n0):
                if not (isinstance(c, int) and c < 2):
                    sp.wait_ge(xT_turned, c - 1)
                sp.dma_start(x_in[:, b], x[ds(n0, NB), :].rearrange("(j p) d -> p j d", p=P)).then_inc(x_landed[b], 16)

            def store_rows(c, b, n0):
                sp.wait_ge(proj_act, c + 1)
                sp.wait_ge(proj_dve, c + 1)
                sp.dma_start(kv_rows[ds(n0, NB), :].rearrange("(j p) d -> p j d", p=P), proj[:, b, :, 0:KV]).then_inc(kv_stored[b], 16)
                sp.dma_start(q_rows[ds(n0, NB), :].rearrange("(j p) d -> p j d", p=P), proj[:, b, :, KV:KV + D]).then_inc(q_stored[b], 16)

            load_x(0, 0, 0)
            load_x(1, 1, NB)
            for r in range(RT):
                sp.wait_ge(relb_cast, r + 1)
                sp.dma_start(rel_rows[first_row(r):first_row(r) + rows_of(r), :], rel_b[0:rows_of(r), r, :]).then_inc(rel_stored, 16)
            sp.wait_ge(consts_cast, 1)
            sp.dma_start(q_rows[N:NPAD, :], zeros[:, :]).then_inc(pad_stored, 16)
            with sp.Fori(0, CHUNKS // 2 - 1) as i:
                for b in range(2):
                    store_rows(i * 2 + b, b, (i * 2 + b) * NB)
                    load_x(i * 2 + b + 2, b, (i * 2 + b + 2) * NB)
            store_rows(CHUNKS - 2, 0, (CHUNKS - 2) * NB)
            load_x(CHUNKS, 0, NLAST)
            store_rows(CHUNKS - 1, 1, (CHUNKS - 1) * NB)
            sp.wait_ge(kv_stored[1], 16 * (CHUNKS // 2))
            sp.wait_ge(q_stored[1], 16 * (CHUNKS // 2))
            store_rows(CHUNKS, 0, NLAST)

            sp.wait_ge(rel_stored, 16 * RT)
            sp.wait_ge(pad_stored, 16)
            sp.wait_ge(q_stored[0], 16 * (CHUNKS // 2 + 1))
            sp.wait_ge(base_landed, 32)
            sp.wait_ge(xT_turned, CHUNKS + 1)

            def edge_loads(i, first=False, last=False):
                for u in range(UNROLL):
                    _, s, n = group(i, u)
                    b = s % 2
                    e0 = LAST0 if last and u == UNROLL - 1 else n * EG
                    if not (first and u < 2):
                        sp.wait_ge(far_done, n - 1)
                    row = rel_rows[ds(n, 1), :]
                    sp.dma_start(relb[:, b, :], row.to_broadcast([WIN, EG])).then_inc(relb_landed[s], 16)
                    if not first:
                        sp.wait_ge(eaT_ready, n - UNROLL + 1)
                    part = edge_attr[ds(e0, EG), :].rearrange("(p j) d -> p j d", j=TILES)
                    sp.dma_start(ea[:, s], part).then_inc(ea_landed[s], 16)
                    node = sp.value_load(base_i[0:1, ds(n, 1)], min_val=0, max_val=N - 1)
                    if not (first and u < 2):
                        sp.wait_ge(qe_ready, n - 1)
                    sp.dma_start(qwin[:, b, :], q_rows[ds(node, WIN), :]).then_inc(qwin_landed[s], 16)

            edge_loads(0, first=True)
            with sp.Fori(1, TURNS - 1) as i:
                edge_loads(i)
            edge_loads(TURNS - 1, last=True)

            def stray_loads(g, last):
                sp.wait_ge(st_begun, g + 1)
                e0 = LAST0 if last else g * EG
                sp.dma_start(ea[:, 0], edge_attr[ds(e0, EG), :].rearrange("(p j) d -> p j d", j=TILES)).then_inc(st_loaded, 16)
                for k, ends in enumerate((src, dst)):
                    sp.dma_start(st_ends[:, k, :], ends[ds(e0, EG)].rearrange("(p j) -> p j", j=TILES)).then_inc(st_loaded, 16)

            strays(sp, stray_loads)

            def store_out(c, b, n0):
                sp.wait_ge(o_done, c + 1)
                sp.dma_start(out[ds(n0, NB), :].rearrange("(j p) d -> p j d", p=P), proj[:, b, :, 0:D]).then_inc(out_stored[b], 16)

            with sp.Fori(0, CHUNKS // 2) as i:
                for b in range(2):
                    store_out(i * 2 + b, b, (i * 2 + b) * NB)
            sp.wait_ge(out_stored[1], 16 * (CHUNKS // 2))
            store_out(CHUNKS, 0, NLAST)
            sp.wait_ge(out_stored[0], 16 * (CHUNKS // 2 + 1))
            sp.wait_ge(out_stored[1], 16 * (CHUNKS // 2))

        @block.gpsimd
        def _(pool):
            nc.gpsimd.memset(ident[:, :], 0.0).then_inc(ident_zero, 1)
            pool.wait_ge(ident_zero, 1)
            nc.gpsimd.affine_select(out=ident[:, :], in_=ident[:, :], compare_op=ALU.not_equal, fill=1.0, base=0,
                                    pattern=[[-1, P]], channel_multiplier=1).then_inc(consts_made, 1)
            nc.gpsimd.iota(iota_i[:, :], pattern=[[1, HALF]], base=0, channel_multiplier=0).then_inc(consts_made, 1)
            nc.gpsimd.iota(place_i[:, :], pattern=[[0, 1]], base=0, channel_multiplier=1).then_inc(consts_made, 1)

            def keep_xT(c, b, n0):
                pool.wait_ge(xT_copied, c + 1)
                nc.gpsimd.tensor_copy(xT[:, ds(n0, NB)], eaT[:, b, :]).then_inc(xT_kept, 1)

            with pool.Fori(0, CHUNKS // 2) as i:
                for b in range(2):
                    keep_xT(i * 2 + b, b, (i * 2 + b) * NB)
            pool.wait_ge(xT_kept, CHUNKS)
            keep_xT(CHUNKS, 0, NLAST)

            pool.wait_ge(kv_stored[0], 16 * (CHUNKS // 2 + 1))
            pool.wait_ge(kv_stored[1], 16 * (CHUNKS // 2))
            pool.wait_ge(q_stored[0], 16 * (CHUNKS // 2 + 1))
            pool.wait_ge(q_stored[1], 16 * (CHUNKS // 2))

            def gathers(i, first=False):
                for u in range(UNROLL):
                    _, s, n = group(i, u)
                    pool.wait_ge(idx_ready, n + 1)
                    if not first:
                        pool.wait_ge(agg_ready, n - UNROLL + 1)
                    pool.sem_inc(gather_begun, 1)
                    for j in range(TILES):
                        pool.indirect_dma_start(
                            out=kv[:, s, j, :], out_offset=None, in_=kv_rows,
                            in_offset=bass.IndirectOffsetOnAxis(ap=idx[:, s, j:j + 1], axis=0),
                        ).then_inc(kv_landed[s], 16)

            gathers(0, first=True)
            with pool.Fori(1, TURNS) as i:
                gathers(i)

            def stray_gathers(g, last):
                pool.wait_ge(st_loaded, 48 * (g + 1))
                pool.sem_inc(st_gathering, 1)
                for j in range(TILES):
                    for rows, k, to in ((kv_rows, 0, kv[:, 0, j, :]), (q_rows, 1, st_q[:, j, :])):
                        pool.indirect_dma_start(
                            out=to, out_offset=None, in_=rows,
                            in_offset=bass.IndirectOffsetOnAxis(ap=st_ends[:, k, j:j + 1], axis=0),
                        ).then_inc(st_gathered, 16)

            strays(pool, stray_gathers)

            def residual(k, n0):
                pool.wait_ge(att_done, k + 1)
                h = acc[:, 0, ds(n0, HC)]
                nc.gpsimd.tensor_tensor(h, h, xT[:, ds(n0, HC)], ALU.add).then_inc(h_done, 1)

            with pool.Fori(0, HN) as k:
                residual(k, k * HC)

            def add_x(c, b, n0):
                pool.wait_ge(y1_done, c + 1)
                nc.gpsimd.tensor_tensor(ea[:, b].rearrange("p j d -> p (j d)"), eaT[:, b, :], xT[:, ds(n0, NB)], ALU.add).then_inc(y_done, 1)

            def add_pair(c, b, n0):
                pool.wait_ge(yT_ready, c - 1)
                add_x(c, b, n0)

            for b in range(2):
                add_x(b, b, b * NB)
            with pool.Fori(1, CHUNKS // 2) as i:
                for b in range(2):
                    add_pair(i * 2 + b, b, (i * 2 + b) * NB)
            add_pair(CHUNKS, 0, NLAST)

        @block.scalar
        def _(act):
            def proj_half(c, b):
                act.wait_ge(proj_ready, c + 1)
                for j in range(2):
                    last = nc.scalar.copy(proj[:, b, j, :], proj_ps[j][:, 0:KV + D])
                last.then_inc(proj_act, 1)

            def proj_next(c, b, turn):
                act.wait_ge(kv_stored[b], 16 * turn)
                act.wait_ge(q_stored[b], 16 * turn)
                proj_half(c, b)

            def clear_sums(c):
                nc.scalar.copy(acc_flat[:, ds(c * CLEAR, CLEAR)], zero_col[:, :].to_broadcast([P, CLEAR])).then_inc(acc_clear, 1)

            act.wait_ge(tab_turned, 2 * RT)
            act.wait_ge(inside_done, RT)
            act.wait_ge(rel_stored, 16 * RT)
            act.wait_ge(consts_cast, 1)
            for b in range(2):
                proj_half(b, b)
                clear_sums(b)
            with act.Fori(1, CHUNKS // 2) as i:
                for b in range(2):
                    proj_next(i * 2 + b, b, i)
                    clear_sums(i * 2 + b)
            proj_next(CHUNKS, 0, CHUNKS // 2)

            def ea_copy(i, u, k):
                _, _, n = group(i, u, k)
                act.wait_ge(eaT_ready, n + 1)
                if not (isinstance(n, int) and n < 2):
                    act.wait_ge(eh_ready, n - 1)
                nc.scalar.copy(eaT[:, (u + k) % 2, :], eaT_ps[(u + k) % 2][:, :]).then_inc(eaT_copied, 1)

            def onehot_columns(i, u, k):
                t, s, n = group(i, u, k)
                act.wait_ge(relb_landed[s], 16 * (t + 1))
                if not (isinstance(n, int) and n < 1):
                    act.wait_ge(ohT_ready, n)
                nc.scalar.activation(far[:, :], relb[:, s % 2, :], ACT.Abs, bias=minus_p[0:WIN, :]).then_inc(far_done, 1)
                if not (isinstance(n, int) and n < 2):
                    act.wait_ge(qe_ready, n - 1)
                act.wait_ge(far_done, n + 1)
                nc.scalar.activation(ohT[:, (u + k) % 2, :], far[:, :], ACT.Relu, scale=-1.0, bias=one_col[0:WIN, :]).then_inc(ohT_ready, 1)

            def indices(i, u, k):
                t, s, n = group(i, u, k)
                if not (isinstance(n, int) and n < UNROLL):
                    act.wait_ge(kv_landed[s], 16 * TILES * t)
                nc.scalar.copy(idx[:, s, :], src_t[:, ds(n, 1), :].rearrange("p a j -> p (a j)")).then_inc(idx_ready, 1)

            def exponent(i, u):
                _, _, n = group(i, u)
                act.wait_ge(clip_done, n + 1)
                if not (isinstance(n, int) and n < 1):
                    act.wait_ge(agg_ready, n)
                wide = sclip[:, u % 2, :].unsqueeze(2).to_broadcast([P, TILES * HEADS, DH])
                nc.scalar.activation(score[:, :, :], wide, ACT.Exp).then_inc(exp_done, 1)

            def edge_turn(i):
                for u in range(UNROLL):
                    left = NG - 1 - group(i, u)[2] if isinstance(i, int) else UNROLL
                    if left >= 1:
                        ea_copy(i, u, 1)
                    exponent(i, u)
                    if left >= 2:
                        onehot_columns(i, u, 2)
                    if left >= UNROLL:
                        indices(i, u, UNROLL)

            act.wait_ge(xT_kept, CHUNKS + 1)
            act.wait_ge(tab_copied, 2 * RT)
            act.wait_ge(src_pad, 1)
            act.wait_ge(consts_cast, 1)
            for u in range(UNROLL):
                indices(0, u, 0)
            onehot_columns(0, 0, 0)
            ea_copy(0, 0, 0)
            onehot_columns(0, 0, 1)
            edge_turn(0)
            with act.Fori(1, TURNS - 1) as i:
                edge_turn(i)
            edge_turn(TURNS - 1)

            def stray_activations(g, last):
                act.wait_ge(st_turned, g + 1)
                nc.scalar.copy(eaT[:, 0, :], eaT_ps[0][:, :]).then_inc(st_eaT, 1)
                act.wait_ge(st_clip, g + 1)
                wide = sclip[:, 1, :].unsqueeze(2).to_broadcast([P, TILES * HEADS, DH])
                nc.scalar.activation(score[:, :, :], wide, ACT.Exp).then_inc(st_exp, 1)
                act.wait_ge(st_added, (g + 1) * SWEEP)

            strays(act, stray_activations)

            act.wait_ge(agg_added, NG)
            with act.Fori(0, HN) as k:
                z = acc[:, 1, ds(k * HC, HC)]
                nc.scalar.activation(z, z, ACT.Identity, bias=eps_attn[:, :]).then_inc(z_done, 1)
            act.wait_ge(bn_step, 1)
            nc.scalar.activation(bn[:, 2:3], bn[:, 1:2], ACT.Sqrt, bias=eps_bn[:, :]).then_inc(bn_std, 1)

            def normalise(c, b, stored=None):
                act.wait_ge(yaggr_done, c + 1)
                nc.scalar.activation(ystd[:, b, :], ymv[:, b, :, 1:2].rearrange("p j a -> p (j a)"), ACT.Sqrt, bias=eps_ln[:, :]).then_inc(ystd_done, 1)
                act.wait_ge(ynorm_known, c + 1)
                if stored is not None:
                    act.wait_ge(out_stored[b], stored)
                for j in range(TILES):
                    last = nc.scalar.activation(proj[:, b, j, 0:D], eaT_ps[b][:, j * P:(j + 1) * P], ACT.Identity,
                                                scale=yrec[:, b, j:j + 1], bias=ymr[:, b, j:j + 1])
                last.then_inc(o_done, 1)

            for b in range(2):
                normalise(b, b)
            with act.Fori(1, CHUNKS // 2) as i:
                for b in range(2):
                    normalise(i * 2 + b, b, 16 * i)
            normalise(CHUNKS, 0, 16 * (CHUNKS // 2))

        @block.tensor
        def _(pe):
            pe.wait_ge(consts_made, 3)
            tabs = [(rel_f, r, rel_done, r + 1) for r in range(RT)] + [(src_f, r, cast_done, RT + r + 1) for r in range(RT)]
            for k, (table_f, r, made, count) in enumerate(tabs):
                R = rows_of(r)
                pe.wait_ge(made, count)
                if k >= 2:
                    pe.wait_ge(tab_copied, k - 1)
                for j in range(TILES):
                    last = pe.transpose(agg_ps[k % 2][:, j * P:j * P + R], table_f[0:R, r, j::TILES], ident[0:R, 0:R])
                last.then_inc(tab_turned, 1)
            pe.wait_ge(inside_done, RT)
            pe.wait_ge(consts_cast, 1)
            pe.wait_ge(tab_copied, 2 * RT)
            pe.matmul(agg_ps[0][0:1, 0:RT], ones[:, :], inside[:, :], start=True, stop=True).then_inc(inside_sum, 1)

            def turn_x(c, b, landed):
                pe.wait_ge(x_landed[b], 16 * landed)
                if not (isinstance(c, int) and c < 2):
                    pe.wait_ge(xT_copied, c - 1)
                for j in range(NB // P):
                    last = pe.transpose(eaT_ps[b][:, j * P:(j + 1) * P], x_in[:, b, j, :], ident[:, :])
                last.then_inc(xT_turned, 1)

            def project(c, b):
                pe.wait_ge(xT_copied, c + 1)
                if not (isinstance(c, int) and c < 1):
                    pe.wait_ge(proj_act, c)
                    pe.wait_ge(proj_dve, c)
                for j in range(NB // P):
                    last = pe.matmul(proj_ps[j][:, 0:KV + D], eaT[:, b, j * P:(j + 1) * P], w_all[:, :], start=True, stop=True)
                last.then_inc(proj_ready, 1)

            def node_turn(i):
                for b in range(2):
                    project(i * 2 + b, b)
                    turn_x(i * 2 + b + 2, b, i + 2)

            pe.wait_ge(w_landed, 16 * 6)
            pe.wait_ge(wq_scaled, 1)
            turn_x(0, 0, 1)
            turn_x(1, 1, 1)
            node_turn(0)
            with pe.Fori(1, CHUNKS // 2 - 1) as i:
                node_turn(i)
            project(CHUNKS - 2, 0)
            turn_x(CHUNKS, 0, CHUNKS // 2 + 1)
            project(CHUNKS - 1, 1)
            project(CHUNKS, 0)

            def ea_turn(i, u, k):
                t, s, n = group(i, u, k)
                pe.wait_ge(ea_landed[s], 16 * (t + 1))
                if not (isinstance(n, int) and n < 2):
                    pe.wait_ge(eaT_copied, n - 1)
                for j in range(TILES):
                    last = pe.transpose(eaT_ps[s % 2][:, j * P:(j + 1) * P], ea[:, s, j, :], ident[:, :])
                last.then_inc(eaT_ready, 1)

            def spread_q(i, u, k):
                t, s, n = group(i, u, k)
                pe.wait_ge(ohT_ready, n + 1)
                pe.wait_ge(qwin_landed[s], 16 * (t + 1))
                if not (isinstance(n, int) and n < 2):
                    pe.wait_ge(kq_done, n - 1)
                for j in range(TILES):
                    last = pe.matmul(qe_ps[s % 2][:, j * P:(j + 1) * P], ohT[:, s % 2, j * P:(j + 1) * P], qwin[:, s % 2, :], start=True, stop=True)
                last.then_inc(qe_ready, 1)

            def edge_product(i, u, k):
                t, s, n = group(i, u, k)
                pe.wait_ge(eaT_copied, n + 1)
                if not (isinstance(n, int) and n < 2):
                    pe.wait_ge(prod_done, n - 1)
                for j in range(TILES):
                    last = pe.matmul(eh_ps[s % 2][:, j * P:(j + 1) * P], eaT[:, s % 2, j * P:(j + 1) * P], we_sb[:, :], start=True, stop=True)
                last.then_inc(eh_ready, 1)

            def sum_window(i, u):
                t, s, n = group(i, u)
                b = s % 2
                pe.wait_ge(onehot_done, n + 1)
                pe.wait_ge(msg_done, n + 1)
                if not (isinstance(n, int) and n < 2):
                    pe.wait_ge(agg_added, n - 1)
                for j in range(TILES):
                    pe.matmul(agg_ps[b][:, 0:WIN], kv[:, s, j, D:KV], onehot[:, b, j, :], start=(j == 0), stop=(j == TILES - 1))
                for j in range(TILES):
                    wide = score[:, j * HEADS:(j + 1) * HEADS, :].rearrange("p h d -> p (h d)")
                    last = pe.matmul(agg_ps[b][:, WIN:2 * WIN], wide, onehot[:, b, j, :], start=(j == 0), stop=(j == TILES - 1))
                last.then_inc(agg_ready, 1)

            def edge_turn(i, last=False):
                for u in range(UNROLL):
                    if not (last and u == UNROLL - 1):
                        ea_turn(i, u, 1)
                        spread_q(i, u, 1)
                        edge_product(i, u, 1)
                    sum_window(i, u)

            pe.wait_ge(proj_act, CHUNKS + 1)
            pe.wait_ge(proj_dve, CHUNKS + 1)
            pe.wait_ge(stray_known, 1)
            ea_turn(0, 0, 0)
            spread_q(0, 0, 0)
            edge_product(0, 0, 0)
            edge_turn(0)
            with pe.Fori(1, TURNS - 1) as i:
                edge_turn(i)
            edge_turn(TURNS - 1, last=True)

            def stray_products(g, last):
                pe.wait_ge(st_loaded, 48 * (g + 1))
                for j in range(TILES):
                    op = pe.transpose(eaT_ps[0][:, j * P:(j + 1) * P], ea[:, 0, j, :], ident[:, :])
                op.then_inc(st_turned, 1)
                pe.wait_ge(st_eaT, g + 1)
                for j in range(TILES):
                    op = pe.matmul(eh_ps[0][:, j * P:(j + 1) * P], eaT[:, 0, j * P:(j + 1) * P], we_sb[:, :], start=True, stop=True)
                op.then_inc(st_eh, 1)

                def sweep(v):
                    pe.wait_ge(st_onehots, g * SWEEP + v + 1)
                    for j in range(TILES):
                        pe.matmul(agg_ps[0][:, 0:2 * HALF], kv[:, 0, j, D:KV], st_onehot[:, j, :], start=(j == 0), stop=(j == TILES - 1))
                    for j in range(TILES):
                        wide = score[:, j * HEADS:(j + 1) * HEADS, :].rearrange("p h d -> p (h d)")
                        op = pe.matmul(agg_ps[1][:, 0:2 * HALF], wide, st_onehot[:, j, :], start=(j == 0), stop=(j == TILES - 1))
                    op.then_inc(st_summed, 1)

                with pe.Fori(0, SWEEP) as v:
                    sweep(v)

            strays(pe, stray_products)

            def turn_y(c, b):
                pe.wait_ge(y_done, c + 1)
                if not (isinstance(c, int) and c < 2):
                    pe.wait_ge(o_done, c - 1)
                for j in range(NB // P):
                    last = pe.transpose(eaT_ps[b][:, j * P:(j + 1) * P], ea[:, b, j, :], ident[:, :])
                last.then_inc(yT_ready, 1)

            for b in range(2):
                turn_y(b, b)
            with pe.Fori(1, CHUNKS // 2) as i:
                for b in range(2):
                    turn_y(i * 2 + b, b)
            turn_y(CHUNKS, 0)

        @block.vector
        def _(dve):
            nc.vector.memset(ones[:, :], 1.0)
            nc.vector.memset(one_col[:, :], 1.0)
            nc.vector.memset(zero_col[:, :], 0.0)
            nc.vector.memset(zeros[:, :], 0.0)
            nc.vector.memset(eps_attn[:, :], ATTN_EPS)
            nc.vector.memset(eps_bn[:, :], BN_EPS)
            nc.vector.memset(eps_ln[:, :], LN_EPS)
            nc.vector.memset(inside[:, :], 0.0)
            nc.vector.memset(src_t[:, NG:, :], 0.0).then_inc(src_pad, 1)
            dve.wait_ge(consts_made, 3)
            nc.vector.tensor_copy(iota[:, :], iota_i[:, :])
            nc.vector.tensor_scalar(minus_p[:, :], place_i[:, :], -1.0, None, ALU.mult).then_inc(consts_cast, 1)

            dve.wait_ge(dst_landed, 16 * RT)
            for r in range(RT):
                R = rows_of(r)
                nc.vector.tensor_copy(dst_f[0:R, r, :], dst_i[0:R, r, :]).then_inc(cast_done, 1)
            for r in range(RT):
                R = rows_of(r)
                first = OLD if r == RT - 1 else 0
                dve.wait_ge(cast_done, r + 1)
                nc.vector.tensor_scalar(rel_f[0:R, r, :], dst_f[0:R, r, :], dst_f[0:R, r, first:first + 1], None, ALU.subtract).then_inc(rel_done, 1)
            for r in range(RT):
                R = rows_of(r)
                dve.wait_ge(rel_done, r + 1)
                tiled = rel_b[0:R, r, :].rearrange("g (j p) -> g p j", j=TILES)
                nc.vector.tensor_copy(tiled, rel_f[0:R, r, :].rearrange("g (p j) -> g p j", j=TILES)).then_inc(relb_cast, 1)
            dve.wait_ge(src_landed, 16 * RT)
            for r in range(RT):
                R = rows_of(r)
                nc.vector.tensor_copy(src_f[0:R, r, :], src_i[0:R, r, :]).then_inc(cast_done, 1)
            for r in range(RT):
                R = rows_of(r)
                new = slice(OLD if r == RT - 1 else 0, EG)
                nc.vector.tensor_scalar(low_f[0:R, r, new], rel_f[0:R, r, new], 0.0, None, ALU.is_ge).then_inc(low_done, 1)
                dve.wait_ge(low_done, r + 1)
                nc.vector.scalar_tensor_tensor(out=dst_f[0:R, r, new], in0=rel_f[0:R, r, new], scalar=float(WIN), in1=low_f[0:R, r, new],
                                               op0=ALU.is_lt, op1=ALU.mult, accum_out=inside[0:R, r:r + 1]).then_inc(inside_done, 1)
            for k in range(2 * RT):
                r = k % RT
                R, g0 = rows_of(r), first_row(r)
                dve.wait_ge(tab_turned, k + 1)
                tab = (rel_t if k < RT else src_t)[:, g0:g0 + R, :].rearrange("p g j -> p j g")
                nc.vector.tensor_copy(tab, agg_ps[k % 2][:, :].rearrange("p (j g) -> p j g", j=TILES)[:, :, 0:R]).then_inc(tab_copied, 1)
            dve.wait_ge(tab_copied, 2 * RT)
            nc.vector.memset(rel_t[0:OLD // TILES, NG - 1, :], -1.0).then_inc(rel_masked, 1)
            dve.wait_ge(inside_sum, 1)
            nc.vector.tensor_reduce(inside_all[:, :], agg_ps[0][0:1, 0:RT], AX.X, ALU.add).then_inc(stray_step, 1)
            dve.wait_ge(stray_step, 1)
            nc.vector.tensor_scalar(stray_i[:, :], inside_all[:, :], -1.0, float(E), ALU.mult, ALU.add).then_inc(stray_known, 1)
            dve.wait_ge(w_landed, 16 * 6)
            nc.vector.tensor_scalar(w_all[:, KV:KV + D], w_all[:, KV:KV + D], DH ** -0.5, None, ALU.mult).then_inc(wq_scaled, 1)

            def xT_copy(c, b):
                dve.wait_ge(xT_turned, c + 1)
                if not (isinstance(c, int) and c < 2):
                    dve.wait_ge(proj_ready, c - 1)
                    dve.wait_ge(xT_kept, c - 1)
                nc.vector.tensor_copy(eaT[:, b, :], eaT_ps[b][:, :]).then_inc(xT_copied, 1)

            def proj_half(c, b, turn):
                dve.wait_ge(proj_ready, c + 1)
                if not (isinstance(turn, int) and turn == 0):
                    dve.wait_ge(kv_stored[b], 16 * turn)
                    dve.wait_ge(q_stored[b], 16 * turn)
                for j in (2, 3):
                    last = nc.vector.tensor_copy(proj[:, b, j, :], proj_ps[j][:, 0:KV + D])
                last.then_inc(proj_dve, 1)

            def node_turn(i):
                for b in range(2):
                    proj_half(i * 2 + b, b, i)
                    xT_copy(i * 2 + b + 2, b)

            xT_copy(0, 0)
            xT_copy(1, 1)
            node_turn(0)
            with dve.Fori(1, CHUNKS // 2 - 1) as i:
                node_turn(i)
            proj_half(CHUNKS - 2, 0, CHUNKS // 2 - 1)
            xT_copy(CHUNKS, 0)
            proj_half(CHUNKS - 1, 1, CHUNKS // 2 - 1)
            proj_half(CHUNKS, 0, CHUNKS // 2)

            def add_window(i, u, k):
                t, s, n = group(i, u, k)
                node = dve.value_load(base_i[0:1, ds(n, 1)], min_val=0, max_val=N - 1)
                dve.wait_ge(agg_ready, n + 1)
                if not (isinstance(n, int) and n < 1):
                    dve.wait_ge(agg_added, n)
                nodes = acc[:, :, ds(node, WIN)]
                nc.vector.tensor_tensor(nodes, nodes, agg_ps[s % 2][:, 0:2 * WIN].rearrange("p (a n) -> p a n", a=2), ALU.add).then_inc(agg_added, 1)

            def edge_turn(i, first=False):
                for u in range(UNROLL):
                    t, s, n = group(i, u)
                    b = s % 2
                    dve.wait_ge(kv_landed[s], 16 * TILES * (t + 1))
                    dve.wait_ge(qe_ready, n + 1)
                    qe = qe_ps[b][:, :].rearrange("p (j d) -> p j d", j=TILES)
                    nc.vector.tensor_tensor(kq[:, :, :], kv[:, s, :, 0:D], qe, ALU.mult).then_inc(kq_done, 1)
                    dve.wait_ge(eh_ready, n + 1)
                    dve.wait_ge(kq_done, n + 1)
                    eh = eh_ps[b][:, :].rearrange("p (j d) -> p j d", j=TILES)
                    nc.vector.tensor_tensor(kq[:, :, :], kq[:, :, :], eh, ALU.mult).then_inc(prod_done, 1)
                    dve.wait_ge(prod_done, n + 1)
                    by_head = kq[:, :, :].rearrange("p j (h d) -> p (j h) d", d=DH)
                    nc.vector.tensor_reduce(ssum[:, :], by_head, AX.X, ALU.add).then_inc(ssum_done, 1)
                    dve.wait_ge(ssum_done, n + 1)
                    nc.vector.tensor_scalar(sclip[:, b, :], ssum[:, :], -5.0, 5.0, ALU.max, ALU.min).then_inc(clip_done, 1)
                    places = iota[:, 0:WIN].unsqueeze(1).to_broadcast([P, TILES, WIN])
                    rel = rel_t[:, ds(n, 1), :].rearrange("p a j -> p (a j)").unsqueeze(2).to_broadcast([P, TILES, WIN])
                    nc.vector.tensor_tensor(onehot[:, b], places, rel, ALU.is_equal).then_inc(onehot_done, 1)
                    if not (first and u == 0):
                        add_window(i, u, -1)
                    dve.wait_ge(exp_done, n + 1)
                    v = kv[:, s, :, D:KV]
                    wide = score[:, :, :].rearrange("p (j h) d -> p j (h d)", j=TILES)
                    nc.vector.tensor_tensor(v, v, wide, ALU.mult).then_inc(msg_done, 1)

            dve.wait_ge(pad_stored, 16)
            dve.wait_ge(rel_masked, 1)
            dve.wait_ge(acc_clear, CHUNKS)
            dve.wait_ge(base_landed, 32)
            edge_turn(0, first=True)
            with dve.Fori(1, TURNS) as i:
                edge_turn(i)
            add_window(TURNS - 1, UNROLL - 1, 0)

            def stray_sums(g, last):
                STEPS = 8
                done = g * STEPS
                dve.wait_ge(st_gathered, 16 * 2 * TILES * (g + 1))
                nc.vector.tensor_tensor(kq[:, :, :], kv[:, 0, :, 0:D], st_q, ALU.mult).then_inc(st_step, 1)
                dve.wait_ge(st_eh, g + 1)
                dve.wait_ge(st_step, done + 1)
                nc.vector.tensor_tensor(kq[:, :, :], kq[:, :, :], eh_ps[0][:, :].rearrange("p (j d) -> p j d", j=TILES), ALU.mult).then_inc(st_step, 1)
                dve.wait_ge(st_step, done + 2)
                nc.vector.tensor_reduce(ssum[:, :], kq[:, :, :].rearrange("p j (h d) -> p (j h) d", d=DH), AX.X, ALU.add).then_inc(st_step, 1)
                dve.wait_ge(st_step, done + 3)
                nc.vector.tensor_scalar(sclip[:, 1, :], ssum[:, :], -5.0, 5.0, ALU.max, ALU.min).then_inc(st_clip, 1)
                rel = rel_t[:, ds(g, 1), :].rearrange("p a j -> p (a j)")
                nc.vector.tensor_scalar(st_low, rel, 0.0, None, ALU.is_ge).then_inc(st_step, 1)
                dve.wait_ge(st_step, done + 4)
                nc.vector.scalar_tensor_tensor(out=st_in, in0=rel, scalar=float(WIN), in1=st_low, op0=ALU.is_lt, op1=ALU.mult).then_inc(st_step, 1)
                nc.vector.tensor_scalar(st_key_hi, st_ends[:, 1, :], 1.0, None, ALU.add).then_inc(st_step, 1)
                dve.wait_ge(st_step, done + 6)
                nc.vector.tensor_scalar(st_low, st_in, -1.0, 1.0, ALU.mult, ALU.add).then_inc(st_step, 1)
                dve.wait_ge(st_step, done + 7)
                nc.vector.tensor_tensor(st_in, st_key_hi, st_low, ALU.mult).then_inc(st_step, 1)
                dve.wait_ge(st_step, done + 8)
                if last:
                    nc.vector.memset(st_in[0:OLD // TILES, :], 0.0).then_inc(st_step, 1)
                    dve.wait_ge(st_step, done + 9)
                KEYS = 2 * (SWEEP + 1)
                nc.vector.tensor_scalar(st_key, st_in, -1.0, None, ALU.add).then_inc(st_keyed, 1)
                nc.vector.tensor_scalar(st_key_hi, st_in, -1.0 - HALF, None, ALU.add).then_inc(st_keyed, 1)
                dve.wait_ge(st_exp, g + 1)
                v = kv[:, 0, :, D:KV]
                nc.vector.tensor_tensor(v, v, score[:, :, :].rearrange("p (j h) d -> p j (h d)", j=TILES), ALU.mult).then_inc(st_keyed, 1)

                def sweep(v):
                    n = g * SWEEP + v
                    dve.wait_ge(st_keyed, g * (KEYS + 1) + 2 * v + 3)
                    places = iota[:, 0:HALF].unsqueeze(1).to_broadcast([P, TILES, HALF])
                    for half, key in enumerate((st_key, st_key_hi)):
                        op = nc.vector.tensor_tensor(st_onehot[:, :, half * HALF:(half + 1) * HALF], places,
                                                     key.unsqueeze(2).to_broadcast([P, TILES, HALF]), ALU.is_equal)
                    op.then_inc(st_onehots, 1)
                    dve.wait_ge(st_summed, n + 1)
                    for a in range(2):
                        nodes = acc[:, a, ds(v * 2 * HALF, 2 * HALF)]
                        op = nc.vector.tensor_tensor(nodes, nodes, agg_ps[a][:, 0:2 * HALF], ALU.add)
                    op.then_inc(st_added, 1)
                    dve.wait_ge(st_added, n + 1)
                    for key in (st_key, st_key_hi):
                        nc.vector.tensor_scalar(key, key, -2.0 * HALF, None, ALU.add).then_inc(st_keyed, 1)

                with dve.Fori(0, SWEEP) as v:
                    sweep(v)
                dve.sem_inc(st_begun, 1)

            dve.wait_ge(agg_added, NG)
            dve.sem_inc(st_begun, 1)
            strays(dve, stray_sums)

            def attend(k, n0):
                dve.wait_ge(z_done, k + 1)
                z, m = acc[:, 1, ds(n0, HC)], acc[:, 0, ds(n0, HC)]
                nc.vector.reciprocal(z, z).then_inc(zr_done, 1)
                dve.wait_ge(zr_done, k + 1)
                nc.vector.tensor_tensor(m, m, z, ALU.mult).then_inc(att_done, 1)

            def measure(k, n0):
                dve.wait_ge(h_done, k + 1)
                nc.vector.bn_stats(hstat[:, ds(k, 1), :].rearrange("p a s -> p (a s)"), acc[:, 0, ds(n0, HC)]).then_inc(hstat_done, 1)

            attend(0, 0)
            with dve.Fori(1, HN) as k:
                attend(k, k * HC)
                measure(k - 1, (k - 1) * HC)
            measure(HN - 1, N - HC)
            dve.wait_ge(hstat_done, HN)
            nc.vector.bn_aggr(bn[:, 0:2], hstat[:, :, :].rearrange("p k s -> p (k s)")).then_inc(bn_step, 1)
            dve.wait_ge(bn_std, 1)
            nc.vector.reciprocal(bn[:, 3:4], bn[:, 2:3]).then_inc(bn_step, 1)
            dve.wait_ge(bn_step, 2)
            nc.vector.tensor_tensor(bn[:, 4:5], bn[:, 3:4], gam[:, :], ALU.mult).then_inc(bn_step, 1)
            dve.wait_ge(bn_step, 3)
            nc.vector.tensor_tensor(bn[:, 5:6], bn[:, 0:1], bn[:, 4:5], ALU.mult).then_inc(bn_step, 1)
            dve.wait_ge(bn_step, 4)
            nc.vector.tensor_tensor(bn[:, 6:7], bet[:, :], bn[:, 5:6], ALU.subtract).then_inc(bn_step, 1)
            dve.wait_ge(bn_step, 5)

            def norm_nodes(c, b, n0):
                if not (isinstance(c, int) and c < 2):
                    dve.wait_ge(y_done, c - 1)
                nc.vector.tensor_scalar(eaT[:, b, :], acc[:, 0, ds(n0, NB)], bn[:, 4:5], bn[:, 6:7], ALU.mult, ALU.add).then_inc(y1_done, 1)

            def norm_features(c, b):
                dve.wait_ge(yT_ready, c + 1)
                if not (isinstance(c, int) and c < 2):
                    dve.wait_ge(o_done, c - 1)
                for j in range(TILES):
                    last = nc.vector.bn_stats(ystat[:, b, j, :], eaT_ps[b][:, j * P:(j + 1) * P])
                last.then_inc(ystat_done, 1)
                dve.wait_ge(ystat_done, c + 1)
                dve.sem_inc(aggr_begun, 1)
                for j in range(TILES):
                    last = nc.vector.bn_aggr(ymv[:, b, j, :], ystat[:, b, j, :])
                last.then_inc(yaggr_done, 1)
                dve.wait_ge(ystd_done, c + 1)
                nc.vector.reciprocal(yrec[:, b, :], ystd[:, b, :]).then_inc(yrec_done, 1)
                dve.wait_ge(yrec_done, c + 1)
                nc.vector.scalar_tensor_tensor(out=ymr[:, b, :], in0=ymv[:, b, :, 0:1].rearrange("p j a -> p (j a)"), scalar=-1.0,
                                               in1=yrec[:, b, :], op0=ALU.mult, op1=ALU.mult).then_inc(ynorm_known, 1)

            def node_turn_out(i):
                for b in range(2):
                    norm_features(i * 2 + b, b)
                    norm_nodes(i * 2 + b + 2, b, (i * 2 + b + 2) * NB)

            norm_nodes(0, 0, 0)
            norm_nodes(1, 1, NB)
            node_turn_out(0)
            with dve.Fori(1, CHUNKS // 2 - 1) as i:
                node_turn_out(i)
            norm_features(CHUNKS - 2, 0)
            norm_nodes(CHUNKS, 0, NLAST)
            norm_features(CHUNKS - 1, 1)
            norm_features(CHUNKS, 0)


_INS = ["x", "src", "dst", "edge_attr_128", "L0_gnn_WQ", "L0_gnn_WK", "L0_gnn_WV", "L0_gnn_WE", "L0_gnn_bn_gamma", "L0_gnn_bn_beta"]


def kernel(**inputs):
    import numpy as np
    import concourse.bacc as bacc
    from concourse import mybir
    from concourse.bass_utils import run_bass_kernel_spmd

    nc = bacc.Bacc("TRN2", target_bir_lowering=False, num_devices=1)
    arrays, args = {}, []
    for name in _INS:
        a = np.ascontiguousarray(inputs[name])
        arrays[f"in_{name}"] = a
        args.append(nc.dram_tensor(f"in_{name}", a.shape, mybir.dt.from_np(a.dtype), kind="ExternalInput").ap())
    x = arrays["in_x"]
    args.append(nc.dram_tensor("out", x.shape, mybir.dt.from_np(x.dtype), kind="ExternalOutput").ap())
    build(nc, *args)
    result = run_bass_kernel_spmd(nc, [arrays], core_ids=[0])
    return result.results[0]["out"]
```

```python
P = 128
HEADS = 8
TILES = 4
EG = P * TILES
WIN = 64
UNROLL = 4
NB = 512
HALF = 128
BN_EPS = 1e-5
ATTN_EPS = 1e-6
LN_EPS = 1e-5


def build(nc, x, src, dst, edge_attr, wq, wk, wv, we, gamma, beta, out):
    from contextlib import ExitStack

    import concourse.bass as bass
    from concourse import mybir

    F32, I32, BF16 = mybir.dt.float32, mybir.dt.int32, mybir.dt.bfloat16
    ALU = mybir.AluOpType
    ACT = mybir.ActivationFunctionType
    AX = mybir.AxisListType
    ds = bass.ds

    N, D = x.shape
    E = src.shape[0]
    DH = D // HEADS
    KV = 2 * D
    WHOLE = E // EG
    TAIL = E - WHOLE * EG
    NG = WHOLE + 1
    TURNS = NG // UNROLL
    LAST0 = E - EG
    OLD = EG - TAIL
    NPAD = N + WIN
    assert D == P and NG % UNROLL == 0 and 0 < TAIL < EG and OLD % TILES == 0
    RT = 4
    ROWS = NG // RT
    MASK0 = (ROWS - 1) // 32 * 32
    assert ROWS * RT == NG and ROWS <= P
    CHUNKS = N // NB
    NTURNS = CHUNKS // UNROLL
    NLAST = N - NB
    assert CHUNKS % UNROLL == 0
    EARLY = 3 * UNROLL
    CLEAR = NPAD // (CHUNKS // 2)
    assert CLEAR * (CHUNKS // 2) == NPAD and CHUNKS - EARLY == CHUNKS // 2
    HC = 500
    HQ = HC // TILES
    HN = N // HC
    assert HN * HC == N and HN % 2 == 1 and HQ <= P
    SWEEP = -(-N // (2 * HALF))
    assert SWEEP * 2 * HALF <= NPAD

    with ExitStack() as ctx:
        def sb(name, shape, dt=F32):
            return ctx.enter_context(nc.sbuf_tensor(name, shape, dt))

        def bank(name):
            return ctx.enter_context(nc.psum_tensor(name, [P, 512], F32))

        def sem(name):
            return ctx.enter_context(nc.semaphore(name))

        kv_rows = nc.dram_tensor("kv_rows", (N, KV), F32).ap()

        eaT_ps = bank("eaT_ps")
        ohT_ps = bank("ohT_ps")
        qw_ps = bank("qw_ps")
        agg_ps = bank("agg_ps")
        qe_ps = [bank(f"qe_ps{b}") for b in range(2)]
        eh_ps = [bank(f"eh_ps{b}") for b in range(2)]
        ohT_b = ohT_ps[:, :].bitcast(BF16)[0:WIN, 0:EG]
        tab_ps = [agg_ps, qw_ps]
        xT_ps = [eaT_ps, ohT_ps]
        proj_ps = [qe_ps, eh_ps]
        st_xT_ps, st_agg_ps = ohT_ps, [agg_ps, qw_ps]
        zT_ps, rT_ps = [eaT_ps, ohT_ps], qe_ps
        yT_ps = eh_ps + [qw_ps, agg_ps]

        xT = sb("xT", [P, NPAD])
        acc = sb("acc", [P, NPAD])
        z_sum = sb("z_sum", [HEADS, NPAD])
        src_t = sb("src_t", [P, NG, TILES])
        rel_t = sb("rel_t", [P, NG, TILES])
        ident = sb("ident", [P, P])
        ident_b = sb("ident_b", [P, P], BF16)
        ones = sb("ones", [P, 1])
        iota = sb("iota", [P, HALF])
        w_kv = sb("w_kv", [P, KV])
        w_q = sb("w_q", [P, D])
        we_sb = sb("we_sb", [P, D])
        gam = sb("gam", [P, 1])
        bet = sb("bet", [P, 1])
        eps_attn = sb("eps_attn", [P, 1])
        eps_bn = sb("eps_bn", [P, 1])
        eps_ln = sb("eps_ln", [P, 1])
        zero_col = sb("zero_col", [P, 1])
        inside = sb("inside", [P, RT])
        inside_all = sb("inside_all", [1, 1])
        stray_i = sb("stray_i", [1, 1], I32)

        def table(k, dt=F32):
            v = acc[:, k * RT * EG:(k + 1) * RT * EG]
            v = v if dt == F32 else v.bitcast(dt)
            return v.rearrange("p (r e) -> p r e", r=RT)

        dst_i, src_i = table(0, I32), table(1, I32)
        dst_f, src_f, rel_f, low_f = table(2), table(3), table(4), table(5)
        assert 6 * RT * EG <= NPAD
        first_i = sb("first_i", [P, RT], I32)
        first_f = sb("first_f", [P, RT])

        ea = sb("ea", [P, UNROLL, TILES, D])
        eaT = sb("eaT", [P, 2, EG])
        xw = sb("xw", [P, 2, WIN])
        node_room = sb("node_room", [P, 2, EG])
        ohT = node_room[0:WIN]
        base_i = node_room[WIN:WIN + 1, 0, 0:NG].bitcast(I32)
        qwin = sb("qwin", [WIN, 2, D])
        idx = sb("idx", [P, UNROLL, TILES], I32)
        kv = sb("kv", [P, UNROLL, TILES, KV])
        kq = sb("kq", [P, TILES, D])
        ssum = sb("ssum", [P, TILES * HEADS])
        sclip = sb("sclip", [P, 2, TILES * HEADS])
        score = sb("score", [P, TILES * HEADS])
        onehot_b = sb("onehot_b", [P, 2, TILES, WIN], BF16)
        onehot = sb("onehot", [P, UNROLL, TILES, WIN])
        x_in = ea
        kv_flat = kv[:, :, :, :].rearrange("p u j d -> p (u j d)")
        o_rows = kv_flat[:, 0:UNROLL * TILES * D].rearrange("p (s j d) -> p s j d", s=UNROLL, j=TILES)
        iota_i = kq[:, :, :].rearrange("p j d -> p (j d)")[:, 0:HALF].bitcast(I32)

        bn = sb("bn", [P, 8])
        stats = onehot[:, :, :, :].rearrange("p b j n -> p (b j n)")
        hstat = stats[:, 0:HN * 6].rearrange("p (k s) -> p k s", s=6)
        ystat = stats[:, HN * 6:(HN + UNROLL * TILES) * 6].rearrange("p (s j a) -> p s j a", s=UNROLL, a=6)
        ymv = sb("ymv", [P, UNROLL, TILES, 2])
        ystd = sb("ystd", [P, UNROLL, TILES])
        yrec = sb("yrec", [P, UNROLL, TILES])
        ymr = sb("ymr", [P, UNROLL, TILES])
        z_rec = sclip
        z_wide = [room.rearrange("p (q d) -> p q d", d=DH) for room in
                  (kq[:, :, :].rearrange("p j d -> p (j d)"), kv_flat[:, 0:EG])]

        consts_made = sem("consts_made")
        consts_cast = sem("consts_cast")
        ident_zero = sem("ident_zero")
        tail_masked = sem("tail_masked")
        xT_padded = sem("xT_padded")
        wkv_landed = sem("wkv_landed")
        w_landed = sem("w_landed")
        wq_scaled = sem("wq_scaled")
        dst_landed = sem("dst_landed")
        src_landed = sem("src_landed")
        first_landed = sem("first_landed")
        base_landed = sem("base_landed")
        first_cast = sem("first_cast")
        dst_cast = sem("dst_cast")
        src_cast = sem("src_cast")
        rel_done = sem("rel_done")
        low_done = sem("low_done")
        inside_done = sem("inside_done")
        tab_turned = sem("tab_turned")
        tab_copied = sem("tab_copied")
        inside_sum = sem("inside_sum")
        stray_step = sem("stray_step")
        stray_known = sem("stray_known")
        msg_clear = sem("msg_clear")
        sco_clear = sem("sco_clear")

        x_landed = [sem(f"x_landed{s}") for s in range(UNROLL)]
        kv_stored = [sem(f"kv_stored{s}") for s in range(UNROLL)]
        xT_turned = sem("xT_turned")
        xT_copied = sem("xT_copied")
        xT_kept = sem("xT_kept")
        proj_ready = sem("proj_ready")
        proj_copied = sem("proj_copied")

        ea_landed = [sem(f"ea_landed{u}") for u in range(UNROLL)]
        kv_landed = [sem(f"kv_landed{u}") for u in range(UNROLL)]
        idx_ready = sem("idx_ready")
        gather_begun = sem("gather_begun")
        eaT_ready = sem("eaT_ready")
        eaT_copied = sem("eaT_copied")
        ohT_ready = sem("ohT_ready")
        ohT_copied = sem("ohT_copied")
        xw_ready = sem("xw_ready")
        qw_ready = sem("qw_ready")
        qw_copied = sem("qw_copied")
        qe_ready = sem("qe_ready")
        eh_ready = sem("eh_ready")
        kq_done = sem("kq_done")
        prod_done = sem("prod_done")
        ssum_done = sem("ssum_done")
        clip_done = sem("clip_done")
        exp_done = sem("exp_done")
        onehot_done = sem("onehot_done")
        onehot_cast = sem("onehot_cast")
        msg_done = sem("msg_done")
        agg_ready = sem("agg_ready")
        agg_added = sem("agg_added")

        st_ends = idx
        st_x = kv[:, 1, :, 0:D]
        st_onehot = kv[:, 2]
        st_low = sclip[:, 0, 0:TILES]
        st_in = sclip[:, 0, TILES:2 * TILES]
        st_key = sclip[:, 0, 2 * TILES:3 * TILES]
        st_key_hi = sclip[:, 0, 3 * TILES:4 * TILES]
        st_begun = sem("st_begun")
        st_loaded = sem("st_loaded")
        st_gathering = sem("st_gathering")
        st_gathered = sem("st_gathered")
        st_turned = sem("st_turned")
        st_copied = sem("st_copied")
        st_products = sem("st_products")
        st_step = sem("st_step")
        st_clip = sem("st_clip")
        st_exp = sem("st_exp")
        st_keyed = sem("st_keyed")
        st_onehots = sem("st_onehots")
        st_summed = sem("st_summed")
        st_added = sem("st_added")

        def strays(eng, group_body):
            eng.wait_ge(stray_known, 1)
            count = eng.value_load(stray_i[0:1, 0:1], min_val=0, max_val=E)
            with eng.If(count > 0):
                with eng.Fori(0, NG - 1) as g:
                    group_body(g, False)
                group_body(NG - 1, True)

        z_ready = sem("z_ready")
        z_turning = sem("z_turning")
        z_turned = sem("z_turned")
        zr_done = sem("zr_done")
        zw_done = sem("zw_done")
        rT_turned = sem("rT_turned")
        att_done = sem("att_done")
        h_done = sem("h_done")
        hstat_done = sem("hstat_done")
        bn_step = sem("bn_step")
        bn_std = sem("bn_std")
        y1_done = sem("y1_done")
        y_done = sem("y_done")
        yT_ready = sem("yT_ready")
        ystat_done = sem("ystat_done")
        aggr_begun = sem("aggr_begun")
        yaggr_done = sem("yaggr_done")
        ystd_done = sem("ystd_done")
        yrec_done = sem("yrec_done")
        ynorm_known = sem("ynorm_known")
        o_done = sem("o_done")
        out_stored = [sem(f"out_stored{s}") for s in range(UNROLL)]

        def group(i, u, k=0):
            t, s = i + (u + k) // UNROLL, (u + k) % UNROLL
            return t, s, t * UNROLL + s

        def early(n, count):
            return isinstance(n, int) and n < count

        def node_rows(rows, n0):
            return rows[ds(n0, NB), :].rearrange("(p j) d -> p j d", j=TILES)

        block = ctx.enter_context(nc.Block())

        @block.sync
        def _(sp):
            def load_x(c, s, n0):
                if not early(c, UNROLL):
                    sp.wait_ge(xT_turned, c - UNROLL + 1)
                sp.dma_start(x_in[:, s], node_rows(x, n0)).then_inc(x_landed[s], 16)

            def store_rows(c, s, n0):
                sp.wait_ge(proj_copied, 2 * (c + 1))
                sp.dma_start(node_rows(kv_rows, n0), kv[:, s]).then_inc(kv_stored[s], 16)

            def load_ends(ends, table_i, landed, tail0, tail_to):
                full = (RT - 1) * ROWS * EG
                sp.dma_start(table_i[0:ROWS, 0:RT - 1, :], ends[0:full].rearrange("(r p e) -> p r e", p=ROWS, e=EG)).then_inc(landed, 16)
                sp.dma_start(table_i[0:ROWS - 1, RT - 1, :], ends[full:WHOLE * EG].rearrange("(p e) -> p e", e=EG)).then_inc(landed, 16)
                sp.dma_start(table_i[ROWS - 1:ROWS, RT - 1, tail_to:EG], ends[tail0:E].rearrange("(a e) -> a e", a=1)).then_inc(landed, 16)

            load_x(0, 0, 0)
            for k, w in enumerate((wk, wv)):
                sp.dma_start(w_kv[:, k * D:(k + 1) * D], w).then_inc(wkv_landed, 16)
            load_x(1, 1, NB)
            load_x(2, 2, 2 * NB)
            load_x(3, 3, 3 * NB)
            with nc.allow_non_contiguous_dma(reason="one word of each group"):
                words = dst[0:WHOLE * EG].rearrange("(g e) -> g e", e=EG)[:, 0:1]
                full = (RT - 1) * ROWS
                sp.dma_start(first_i[0:ROWS, 0:RT - 1], words[0:full, :].rearrange("(r p) a -> p (r a)", p=ROWS)).then_inc(first_landed, 16)
                sp.dma_start(first_i[0:ROWS - 1, RT - 1:RT], words[full:WHOLE, :]).then_inc(first_landed, 16)
                sp.dma_start(first_i[ROWS - 1:ROWS, RT - 1:RT], dst[E - TAIL:E - TAIL + 1].rearrange("(a b) -> a b", a=1)).then_inc(first_landed, 16)
                sp.wait_ge(tail_masked, 1)
                load_ends(dst, dst_i, dst_landed, E - TAIL, OLD)
                load_ends(src, src_i, src_landed, LAST0, 0)
                sp.dma_start(base_i[0:1, 0:WHOLE].rearrange("a (g b) -> a g b", b=1), words.rearrange("(a g) b -> a g b", a=1)).then_inc(base_landed, 16)
                sp.dma_start(base_i[0:1, WHOLE:NG], dst[E - TAIL:E - TAIL + 1].rearrange("(a b) -> a b", a=1)).then_inc(base_landed, 16)
            sp.dma_start(w_q[:, :], wq).then_inc(w_landed, 16)
            sp.dma_start(we_sb[:, :], we).then_inc(w_landed, 16)
            sp.dma_start(gam[:, :], gamma.rearrange("(d a) -> d a", a=1)).then_inc(w_landed, 16)
            sp.dma_start(bet[:, :], beta.rearrange("(d a) -> d a", a=1)).then_inc(w_landed, 16)

            with sp.Fori(0, NTURNS - 1) as i:
                for u in range(UNROLL):
                    c = i * UNROLL + u
                    load_x(c + UNROLL, u, (c + UNROLL) * NB)
                    store_rows(c, u, c * NB)
            load_x(CHUNKS, 0, NLAST)
            for u in range(UNROLL):
                c = CHUNKS - UNROLL + u
                store_rows(c, u, c * NB)
            sp.wait_ge(kv_stored[UNROLL - 1], 16 * NTURNS)
            store_rows(CHUNKS, 0, NLAST)

            def edge_loads(i, last=False):
                for u in range(UNROLL):
                    _, s, n = group(i, u)
                    e0 = LAST0 if last and u == UNROLL - 1 else n * EG
                    if not early(n, UNROLL):
                        sp.wait_ge(eaT_ready, n - UNROLL + 1)
                    part = edge_attr[ds(e0, EG), :].rearrange("(p j) d -> p j d", j=TILES)
                    sp.dma_start(ea[:, s], part).then_inc(ea_landed[s], 16)

            sp.wait_ge(xT_turned, CHUNKS + 1)
            edge_loads(0)
            with sp.Fori(1, TURNS - 1) as i:
                edge_loads(i)
            edge_loads(TURNS - 1, last=True)

            def stray_loads(g, last):
                sp.wait_ge(st_begun, g + 1)
                e0 = LAST0 if last else g * EG
                sp.dma_start(ea[:, 0], edge_attr[ds(e0, EG), :].rearrange("(p j) d -> p j d", j=TILES)).then_inc(st_loaded, 16)
                for k, ends in enumerate((src, dst)):
                    sp.dma_start(st_ends[:, k, :], ends[ds(e0, EG)].rearrange("(p j) -> p j", j=TILES)).then_inc(st_loaded, 16)

            strays(sp, stray_loads)

            def store_out(c, s, n0):
                sp.wait_ge(o_done, c + 1)
                sp.dma_start(node_rows(out, n0), o_rows[:, s]).then_inc(out_stored[s], 16)

            with sp.Fori(0, NTURNS) as i:
                for u in range(UNROLL):
                    store_out(i * UNROLL + u, u, (i * UNROLL + u) * NB)
            sp.wait_ge(out_stored[UNROLL - 1], 16 * NTURNS)
            store_out(CHUNKS, 0, NLAST)
            for s in range(UNROLL):
                sp.wait_ge(out_stored[s], 16 * (NTURNS + (s == 0)))

        @block.gpsimd
        def _(pool):
            nc.gpsimd.memset(ident[:, :], 0.0).then_inc(ident_zero, 1)
            pool.wait_ge(ident_zero, 1)
            nc.gpsimd.affine_select(out=ident[:, :], in_=ident[:, :], compare_op=ALU.not_equal, fill=1.0, base=0,
                                    pattern=[[-1, P]], channel_multiplier=1).then_inc(consts_made, 1)
            nc.gpsimd.iota(iota_i[:, :], pattern=[[1, HALF]], base=0, channel_multiplier=0).then_inc(consts_made, 1)
            nc.gpsimd.memset(xT[:, N:NPAD], 0.0).then_inc(xT_padded, 1)

            def keep_xT(c, b, n0):
                pool.wait_ge(xT_copied, c + 1)
                nodes = xT[:, ds(n0, NB)].rearrange("f (p j) -> f j p", j=TILES)
                nc.gpsimd.tensor_copy(nodes, eaT[:, b, :].rearrange("f (j p) -> f j p", j=TILES)).then_inc(xT_kept, 1)

            for c in range(EARLY):
                keep_xT(c, c % 2, c * NB)
                if c == 0:
                    pool.wait_ge(first_landed, 16 * 3)
                    nc.gpsimd.tensor_copy(first_f[0:ROWS, :], first_i[0:ROWS, :]).then_inc(first_cast, 1)
                    pool.wait_ge(dst_landed, 16 * 3)
                if c < RT:
                    nc.gpsimd.tensor_copy(dst_f[0:ROWS, c, :], dst_i[0:ROWS, c, :]).then_inc(dst_cast, 1)
                if c == RT:
                    pool.wait_ge(src_landed, 16 * 3)
                if RT <= c < 2 * RT:
                    nc.gpsimd.tensor_copy(src_f[0:ROWS, c - RT, :], src_i[0:ROWS, c - RT, :]).then_inc(src_cast, 1)
            with pool.Fori(EARLY // 2, CHUNKS // 2) as i:
                for b in range(2):
                    keep_xT(i * 2 + b, b, (i * 2 + b) * NB)
            pool.wait_ge(xT_kept, CHUNKS)
            keep_xT(CHUNKS, 0, NLAST)

            for s in range(UNROLL):
                pool.wait_ge(kv_stored[s], 16 * (NTURNS + (s == 0)))

            def gathers(i):
                for u in range(UNROLL):
                    _, s, n = group(i, u)
                    pool.wait_ge(idx_ready, n + 1)
                    pool.sem_inc(gather_begun, 1)
                    for j in range(TILES):
                        pool.indirect_dma_start(
                            out=kv[:, s, j, :], out_offset=None, in_=kv_rows,
                            in_offset=bass.IndirectOffsetOnAxis(ap=idx[:, s, j:j + 1], axis=0),
                        ).then_inc(kv_landed[s], 16)

            with pool.Fori(0, TURNS) as i:
                gathers(i)

            def stray_gathers(g, last):
                pool.wait_ge(st_loaded, 48 * (g + 1))
                pool.sem_inc(st_gathering, 1)
                for j in range(TILES):
                    for rows, k, to in ((kv_rows, 0, kv[:, 0, j, :]), (x, 1, st_x[:, j, :])):
                        pool.indirect_dma_start(
                            out=to, out_offset=None, in_=rows,
                            in_offset=bass.IndirectOffsetOnAxis(ap=st_ends[:, k, j:j + 1], axis=0),
                        ).then_inc(st_gathered, 16)

            strays(pool, stray_gathers)

            def residual(k, n0):
                pool.wait_ge(att_done, k + 1)
                h = acc[:, ds(n0, HC)]
                nc.gpsimd.tensor_tensor(h, h, xT[:, ds(n0, HC)], ALU.add).then_inc(h_done, 1)

            with pool.Fori(0, HN) as k:
                residual(k, k * HC)

            def add_x(c, s, n0):
                pool.wait_ge(y1_done, c + 1)
                if not early(c, UNROLL):
                    pool.wait_ge(yT_ready, c - UNROLL + 1)
                nc.gpsimd.tensor_tensor(ea[:, s].rearrange("p j d -> p (j d)"), eaT[:, s % 2, :], xT[:, ds(n0, NB)], ALU.add).then_inc(y_done, 1)

            for s in range(UNROLL):
                add_x(s, s, s * NB)
            with pool.Fori(1, NTURNS) as i:
                for u in range(UNROLL):
                    add_x(i * UNROLL + u, u, (i * UNROLL + u) * NB)
            add_x(CHUNKS, 0, NLAST)

        @block.scalar
        def _(act):
            def proj_copy(c, s, turn):
                if not early(turn, 1):
                    act.wait_ge(kv_stored[s], 16 * turn)
                for half in range(2):
                    act.wait_ge(proj_ready, 2 * c + half + 1)
                    rows = kv[:, s, 2 * half:2 * half + 2, :].rearrange("p j d -> p (j d)")
                    nc.scalar.copy(rows, proj_ps[s % 2][half][:, :]).then_inc(proj_copied, 1)

            def node_turn(i):
                for u in range(UNROLL):
                    proj_copy(i * UNROLL + u, u, i)
                    if u % 2:
                        piece = z_sum[:, ds((i * 2 + u // 2) * CLEAR, CLEAR)]
                        nc.scalar.copy(piece, zero_col[0:HEADS, :].to_broadcast([HEADS, CLEAR])).then_inc(sco_clear, 1)

            act.wait_ge(consts_cast, 1)
            node_turn(0)
            with act.Fori(1, NTURNS) as i:
                node_turn(i)
            proj_copy(CHUNKS, 0, NTURNS)

            def window_x(i, u, k):
                _, s, n = group(i, u, k)
                node = act.value_load(base_i[0:1, ds(n, 1)], min_val=0, max_val=N - 1)
                if not early(n, 2):
                    act.wait_ge(qw_ready, n - 1)
                nc.scalar.copy(xw[:, s % 2, :], xT[:, ds(node, WIN)]).then_inc(xw_ready, 1)

            def copies(i, u, k):
                _, s, n = group(i, u, k)
                b = s % 2
                act.wait_ge(eaT_ready, n + 1)
                if not early(n, 2):
                    act.wait_ge(eh_ready, n - 1)
                nc.scalar.copy(eaT[:, b, :], eaT_ps[:, :]).then_inc(eaT_copied, 1)
                act.wait_ge(ohT_ready, n + 1)
                if not early(n, 2):
                    act.wait_ge(qe_ready, n - 1)
                nc.scalar.copy(ohT[:, b, :], ohT_b).then_inc(ohT_copied, 1)
                nc.scalar.copy(onehot[:, s], onehot_b[:, b]).then_inc(onehot_cast, 1)
                act.wait_ge(qw_ready, n + 1)
                nc.scalar.copy(qwin[:, b, :], qw_ps[0:WIN, 0:D]).then_inc(qw_copied, 1)

            def indices(i, u, k):
                _, s, n = group(i, u, k)
                nc.scalar.copy(idx[:, s, :], src_t[:, ds(n, 1), :].rearrange("p a j -> p (a j)")).then_inc(idx_ready, 1)

            def exponent(i, u):
                _, _, n = group(i, u)
                act.wait_ge(clip_done, n + 1)
                nc.scalar.activation(score[:, :], sclip[:, u % 2, :], ACT.Exp).then_inc(exp_done, 1)

            def edge_turn(i):
                for u in range(UNROLL):
                    left = NG - 1 - group(i, u)[2] if isinstance(i, int) else UNROLL
                    if not early(group(i, u)[2], 1):
                        act.wait_ge(agg_ready, group(i, u)[2])
                    if left >= 3:
                        indices(i, u, 3)
                    exponent(i, u)
                    if left >= 2:
                        copies(i, u, 2)
                    if left >= 3:
                        window_x(i, u, 3)

            act.wait_ge(tab_copied, 2 * RT)
            for u in range(3):
                indices(0, u, 0)
            act.wait_ge(base_landed, 32)
            act.wait_ge(xT_kept, CHUNKS + 1)
            act.wait_ge(xT_padded, 1)
            window_x(0, 0, 0)
            window_x(0, 1, 0)
            copies(0, 0, 0)
            copies(0, 1, 0)
            window_x(0, 2, 0)
            edge_turn(0)
            with act.Fori(1, TURNS - 1) as i:
                edge_turn(i)
            edge_turn(TURNS - 1)

            def stray_activations(g, last):
                act.wait_ge(st_turned, 2 * g + 1)
                nc.scalar.copy(eaT[:, 0, :], eaT_ps[:, :]).then_inc(st_copied, 1)
                act.wait_ge(st_turned, 2 * g + 2)
                nc.scalar.copy(eaT[:, 1, :], st_xT_ps[:, :]).then_inc(st_copied, 1)
                act.wait_ge(st_clip, g + 1)
                nc.scalar.activation(score[:, :], sclip[:, 1, :], ACT.Exp).then_inc(st_exp, 1)
                act.wait_ge(st_added, (g + 1) * SWEEP)

            strays(act, stray_activations)

            def z_copy(k, b, n0):
                if not early(k, 2):
                    act.wait_ge(z_turned, k - 1)
                nc.scalar.activation(eaT[0:HEADS, b, 0:HC], z_sum[:, ds(n0, HC)], ACT.Identity, bias=eps_attn[0:HEADS, :]).then_inc(z_ready, 1)

            def z_spread(k, b):
                act.wait_ge(zr_done, k + 1)
                if not early(k, 2):
                    act.wait_ge(rT_turned, k - 1)
                wide = z_rec[0:HQ, b, :].unsqueeze(2).to_broadcast([HQ, TILES * HEADS, DH])
                nc.scalar.copy(z_wide[b][0:HQ], wide).then_inc(zw_done, 1)

            act.wait_ge(agg_added, NG)
            z_copy(0, 0, 0)
            for k in range(2):
                z_copy(k + 1, (k + 1) % 2, (k + 1) * HC)
                z_spread(k, k)
            with act.Fori(1, HN // 2) as i:
                for b in range(2):
                    k = i * 2 + b
                    z_copy(k + 1, (b + 1) % 2, (k + 1) * HC)
                    z_spread(k, b)
            z_spread(HN - 1, 0)
            act.wait_ge(bn_step, 1)
            nc.scalar.activation(bn[:, 2:3], bn[:, 1:2], ACT.Sqrt, bias=eps_bn[:, :]).then_inc(bn_std, 1)

            def y_std(c, s):
                act.wait_ge(yaggr_done, c + 1)
                nc.scalar.activation(ystd[:, s, :], ymv[:, s, :, 1:2].rearrange("p j a -> p (j a)"), ACT.Sqrt, bias=eps_ln[:, :]).then_inc(ystd_done, 1)

            def normalise(c, s, turn):
                act.wait_ge(ynorm_known, c + 1)
                if not early(turn, 1):
                    act.wait_ge(out_stored[s], 16 * turn)
                for j in range(TILES):
                    last = nc.scalar.activation(o_rows[:, s, j, :], yT_ps[s][:, j * P:(j + 1) * P], ACT.Identity,
                                                scale=yrec[:, s, j:j + 1], bias=ymr[:, s, j:j + 1])
                last.then_inc(o_done, 1)

            def node_turn_out(i):
                for u in range(UNROLL):
                    y_std(i * UNROLL + u, u)
                    if not (u == 0 and early(i, 1)):
                        t, s, c = group(i, u, -1)
                        normalise(c, s, t)

            node_turn_out(0)
            with act.Fori(1, NTURNS) as i:
                node_turn_out(i)
            y_std(CHUNKS, 0)
            normalise(CHUNKS - 1, UNROLL - 1, NTURNS - 1)
            normalise(CHUNKS, 0, NTURNS)

        @block.tensor
        def _(pe):
            def turn_table(k):
                r = k % RT
                table_f, made = (rel_f, rel_done) if k < RT else (src_f, src_cast)
                pe.wait_ge(made, r + 1)
                if k >= 2:
                    pe.wait_ge(tab_copied, k - 1)
                for j in range(TILES):
                    last = pe.transpose(tab_ps[k % 2][:, j * ROWS:(j + 1) * ROWS], table_f[0:ROWS, r, j::TILES], ident[0:ROWS, 0:ROWS])
                last.then_inc(tab_turned, 1)

            def turn_x(c, s, turn):
                pe.wait_ge(x_landed[s], 16 * (turn + 1))
                if not early(c, 2):
                    pe.wait_ge(xT_copied, c - 1)
                for j in range(TILES):
                    last = pe.transpose(xT_ps[s % 2][:, j * P:(j + 1) * P], x_in[:, s, j, :], ident[:, :])
                last.then_inc(xT_turned, 1)

            def project(c, s):
                pe.wait_ge(xT_copied, c + 1)
                for half in range(2):
                    if not early(c, 2):
                        pe.wait_ge(proj_copied, 2 * (c - 2) + half + 1)
                    for j in (2 * half, 2 * half + 1):
                        last = pe.matmul(proj_ps[s % 2][half][:, (j % 2) * KV:(j % 2 + 1) * KV], eaT[:, s % 2, j * P:(j + 1) * P], w_kv[:, :], start=True, stop=True)
                    last.then_inc(proj_ready, 1)

            def node_turn(i, left=UNROLL):
                for u in range(UNROLL):
                    c = i * UNROLL + u
                    project(c, u)
                    t, s, ahead = group(i, u, 2)
                    if u < left:
                        turn_x(ahead, s, t)
                    if isinstance(c, int) and EARLY - RT - 2 <= c < EARLY - 2:
                        turn_table(2 * (c - (EARLY - RT - 2)))
                        turn_table(2 * (c - (EARLY - RT - 2)) + 1)

            pe.wait_ge(consts_made, 1)
            turn_x(0, 0, 0)
            turn_x(1, 1, 0)
            pe.wait_ge(wkv_landed, 16 * 2)
            for i in range(EARLY // UNROLL):
                node_turn(i)
            with pe.Fori(EARLY // UNROLL, NTURNS - 1) as i:
                node_turn(i)
            node_turn(NTURNS - 1, left=3)
            project(CHUNKS, 0)
            pe.wait_ge(inside_done, RT)
            pe.wait_ge(consts_cast, 1)
            pe.wait_ge(tab_copied, 2 * RT)
            pe.matmul(agg_ps[0:1, 0:RT], ones[:, :], inside[:, :], start=True, stop=True).then_inc(inside_sum, 1)

            def turns(i, u, k):
                t, s, n = group(i, u, k)
                pe.wait_ge(ea_landed[s], 16 * (t + 1))
                pe.wait_ge(onehot_done, n + 1)
                pe.wait_ge(xw_ready, n + 1)
                if not early(n, 1):
                    pe.wait_ge(eaT_copied, n)
                    pe.wait_ge(ohT_copied, n)
                    pe.wait_ge(qw_copied, n)
                for j in range(TILES):
                    last = pe.transpose(eaT_ps[:, j * P:(j + 1) * P], ea[:, s, j, :], ident[:, :])
                last.then_inc(eaT_ready, 1)
                for j in range(TILES):
                    last = pe.transpose(ohT_b[:, j * P:(j + 1) * P], onehot_b[:, s % 2, j, :], ident_b[:, :])
                last.then_inc(ohT_ready, 1)
                pe.matmul(qw_ps[0:WIN, 0:D], xw[:, s % 2, :], w_q[:, :], start=True, stop=True).then_inc(qw_ready, 1)

            def spread_q(i, u, k):
                _, s, n = group(i, u, k)
                pe.wait_ge(ohT_copied, n + 1)
                pe.wait_ge(qw_copied, n + 1)
                if not early(n, 2):
                    pe.wait_ge(kq_done, n - 1)
                for j in range(TILES):
                    last = pe.matmul(qe_ps[s % 2][:, j * P:(j + 1) * P], ohT[:, s % 2, j * P:(j + 1) * P], qwin[:, s % 2, :], start=True, stop=True)
                last.then_inc(qe_ready, 1)

            def edge_product(i, u, k):
                _, s, n = group(i, u, k)
                pe.wait_ge(eaT_copied, n + 1)
                if not early(n, 2):
                    pe.wait_ge(prod_done, n - 1)
                for j in range(TILES):
                    last = pe.matmul(eh_ps[s % 2][:, j * P:(j + 1) * P], eaT[:, s % 2, j * P:(j + 1) * P], we_sb[:, :], start=True, stop=True)
                last.then_inc(eh_ready, 1)

            def sum_window(i, u):
                _, s, n = group(i, u)
                pe.wait_ge(onehot_cast, n + 1)
                pe.wait_ge(msg_done, n + 1)
                if not early(n, 1):
                    pe.wait_ge(agg_added, n)
                for j in range(TILES):
                    pe.matmul(agg_ps[:, 0:WIN], kv[:, s, j, D:KV], onehot[:, s, j, :], start=(j == 0), stop=(j == TILES - 1))
                for j in range(TILES):
                    last = pe.matmul(agg_ps[0:HEADS, WIN:2 * WIN], score[:, j * HEADS:(j + 1) * HEADS], onehot[:, s, j, :], start=(j == 0), stop=(j == TILES - 1))
                last.then_inc(agg_ready, 1)

            def edge_turn(i):
                for u in range(UNROLL):
                    left = NG - 1 - group(i, u)[2] if isinstance(i, int) else UNROLL
                    if left >= 2:
                        turns(i, u, 2)
                    if left >= 1:
                        spread_q(i, u, 1)
                        edge_product(i, u, 1)
                    sum_window(i, u)

            pe.wait_ge(proj_copied, 2 * (CHUNKS + 1))
            pe.wait_ge(wq_scaled, 1)
            pe.wait_ge(stray_step, 1)
            turns(0, 0, 0)
            turns(0, 1, 0)
            spread_q(0, 0, 0)
            edge_product(0, 0, 0)
            edge_turn(0)
            with pe.Fori(1, TURNS - 1) as i:
                edge_turn(i)
            edge_turn(TURNS - 1)

            def stray_products(g, last):
                pe.wait_ge(st_loaded, 48 * (g + 1))
                for j in range(TILES):
                    op = pe.transpose(eaT_ps[:, j * P:(j + 1) * P], ea[:, 0, j, :], ident[:, :])
                op.then_inc(st_turned, 1)
                pe.wait_ge(st_gathered, 16 * 2 * TILES * (g + 1))
                for j in range(TILES):
                    op = pe.transpose(st_xT_ps[:, j * P:(j + 1) * P], st_x[:, j, :], ident[:, :])
                op.then_inc(st_turned, 1)
                pe.wait_ge(st_copied, 2 * g + 2)
                for j in range(TILES):
                    pe.matmul(eh_ps[0][:, j * P:(j + 1) * P], eaT[:, 0, j * P:(j + 1) * P], we_sb[:, :], start=True, stop=True)
                for j in range(TILES):
                    op = pe.matmul(qe_ps[0][:, j * P:(j + 1) * P], eaT[:, 1, j * P:(j + 1) * P], w_q[:, :], start=True, stop=True)
                op.then_inc(st_products, 1)

                def sweep(v):
                    pe.wait_ge(st_onehots, g * SWEEP + v + 1)
                    for j in range(TILES):
                        pe.matmul(st_agg_ps[0][:, 0:2 * HALF], kv[:, 0, j, D:KV], st_onehot[:, j, :], start=(j == 0), stop=(j == TILES - 1))
                    for j in range(TILES):
                        op = pe.matmul(st_agg_ps[1][0:HEADS, 0:2 * HALF], score[:, j * HEADS:(j + 1) * HEADS], st_onehot[:, j, :], start=(j == 0), stop=(j == TILES - 1))
                    op.then_inc(st_summed, 1)

                with pe.Fori(0, SWEEP) as v:
                    sweep(v)

            strays(pe, stray_products)

            def turn_z(k, b):
                pe.wait_ge(z_ready, k + 1)
                if not early(k, 2):
                    pe.wait_ge(zr_done, k - 1)
                pe.sem_inc(z_turning, 1)
                for j in range(TILES):
                    last = pe.transpose(zT_ps[b][0:HQ, j * HEADS:(j + 1) * HEADS], eaT[0:HEADS, b, j * HQ:(j + 1) * HQ], ident[0:HEADS, 0:HEADS])
                last.then_inc(z_turned, 1)

            def turn_back(k, b):
                pe.wait_ge(zw_done, k + 1)
                if not early(k, 2):
                    pe.wait_ge(att_done, k - 1)
                for j in range(TILES):
                    quarter = z_wide[b][0:HQ, j * HEADS:(j + 1) * HEADS, :].rearrange("p h d -> p (h d)")
                    last = pe.transpose(rT_ps[b][:, j * HQ:(j + 1) * HQ], quarter, ident[0:HQ, 0:HQ])
                last.then_inc(rT_turned, 1)

            turn_z(0, 0)
            for k in range(2):
                turn_z(k + 1, (k + 1) % 2)
                turn_back(k, k)
            with pe.Fori(1, HN // 2) as i:
                for b in range(2):
                    turn_z(i * 2 + b + 1, (b + 1) % 2)
                    turn_back(i * 2 + b, b)
            turn_back(HN - 1, 0)

            def turn_y(c, s):
                pe.wait_ge(y_done, c + 1)
                if not early(c, UNROLL):
                    pe.wait_ge(o_done, c - UNROLL + 1)
                nodes = ea[:, s].rearrange("f j d -> f (j d)")
                for j in range(TILES):
                    last = pe.transpose(yT_ps[s][:, j * P:(j + 1) * P], nodes[:, j::TILES], ident[:, :])
                last.then_inc(yT_ready, 1)

            for s in range(UNROLL):
                turn_y(s, s)
            with pe.Fori(1, NTURNS) as i:
                for u in range(UNROLL):
                    turn_y(i * UNROLL + u, u)
            turn_y(CHUNKS, 0)

        @block.vector
        def _(dve):
            nc.vector.memset(dst_i[MASK0:ROWS, RT - 1, :], -(1 << 20)).then_inc(tail_masked, 1)
            nc.vector.memset(zero_col[:, :], 0.0)
            nc.vector.memset(ones[:, :], 1.0)
            nc.vector.memset(eps_attn[:, :], ATTN_EPS)
            nc.vector.memset(eps_bn[:, :], BN_EPS)
            nc.vector.memset(eps_ln[:, :], LN_EPS)
            nc.vector.memset(inside[:, :], 0.0)
            dve.wait_ge(consts_made, 2)
            nc.vector.tensor_copy(ident_b[:, :], ident[:, :])
            nc.vector.tensor_copy(iota[:, :], iota_i[:, :]).then_inc(consts_cast, 1)

            def xT_copy(c, b):
                dve.wait_ge(xT_turned, c + 1)
                if not early(c, 2):
                    dve.wait_ge(proj_ready, 2 * (c - 1))
                    dve.wait_ge(xT_kept, c - 1)
                nc.vector.tensor_copy(eaT[:, b, :], xT_ps[b][:, :]).then_inc(xT_copied, 1)

            def relative(r):
                dve.wait_ge(dst_cast, r + 1)
                rel = rel_f[0:ROWS, r, :]
                nc.vector.tensor_scalar(rel, dst_f[0:ROWS, r, :], first_f[0:ROWS, r:r + 1], None, ALU.subtract).then_inc(rel_done, 1)
                dve.wait_ge(rel_done, r + 1)
                nc.vector.tensor_scalar(low_f[0:ROWS, r, :], rel, 0.0, None, ALU.is_ge).then_inc(low_done, 1)
                dve.wait_ge(low_done, r + 1)
                nc.vector.scalar_tensor_tensor(out=dst_f[0:ROWS, r, :], in0=rel, scalar=float(WIN), in1=low_f[0:ROWS, r, :],
                                               op0=ALU.is_lt, op1=ALU.mult, accum_out=inside[0:ROWS, r:r + 1]).then_inc(inside_done, 1)

            def table_copy(k):
                g0 = k % RT * ROWS
                dve.wait_ge(tab_turned, k + 1)
                tab = (rel_t if k < RT else src_t)[:, g0:g0 + ROWS, :].rearrange("p g j -> p j g")
                nc.vector.tensor_copy(tab, tab_ps[k % 2][:, 0:TILES * ROWS].rearrange("p (j g) -> p j g", j=TILES)).then_inc(tab_copied, 1)

            for c in range(EARLY - 2 * RT):
                xT_copy(c, c % 2)
            dve.wait_ge(first_cast, 1)
            for r in range(RT):
                relative(r)
                xT_copy(EARLY - 2 * RT + r, r % 2)
            for r in range(RT):
                table_copy(2 * r)
                table_copy(2 * r + 1)
                xT_copy(EARLY - RT + r, r % 2)
            with dve.Fori(EARLY // 2, CHUNKS // 2) as i:
                for b in range(2):
                    c = i * 2 + b
                    xT_copy(c, b)
                    nc.vector.tensor_copy(acc[:, ds((c - EARLY) * CLEAR, CLEAR)], zero_col[:, :].to_broadcast([P, CLEAR])).then_inc(msg_clear, 1)
            xT_copy(CHUNKS, 0)
            dve.wait_ge(w_landed, 16 * 4)
            nc.vector.tensor_scalar(w_q[:, :], w_q[:, :], DH ** -0.5, None, ALU.mult).then_inc(wq_scaled, 1)

            def one_hot(i, u, k):
                _, s, n = group(i, u, k)
                if not early(n, 2):
                    dve.wait_ge(onehot_cast, n - 1)
                places = iota[:, 0:WIN].unsqueeze(1).to_broadcast([P, TILES, WIN])
                rel = rel_t[:, ds(n, 1), :].rearrange("p a j -> p (a j)").unsqueeze(2).to_broadcast([P, TILES, WIN])
                nc.vector.tensor_tensor(onehot_b[:, s % 2], places, rel, ALU.is_equal).then_inc(onehot_done, 1)

            def window_of(i, u, k):
                _, s, n = group(i, u, k)
                return dve.value_load(base_i[0:1, ds(n, 1)], min_val=0, max_val=N - 1)

            def add_window(i, u, k, node):
                _, s, n = group(i, u, k)
                dve.wait_ge(agg_ready, n + 1)
                if not early(n, 1):
                    dve.wait_ge(agg_added, n)
                nodes, heads = acc[:, ds(node, WIN)], z_sum[:, ds(node, WIN)]
                nc.vector.tensor_tensor(nodes, nodes, agg_ps[:, 0:WIN], ALU.add)
                nc.vector.tensor_tensor(heads, heads, agg_ps[0:HEADS, WIN:2 * WIN], ALU.add).then_inc(agg_added, 1)

            def weigh(s, done):
                v = kv[:, s, :, D:KV].rearrange("p j (h d) -> p j h d", d=DH)
                wide = score[:, :].rearrange("p (j h) -> p j h", j=TILES).unsqueeze(3).to_broadcast([P, TILES, HEADS, DH])
                nc.vector.tensor_tensor(v, v, wide, ALU.mult).then_inc(done, 1)

            def edge_turn(i):
                for u in range(UNROLL):
                    t, s, n = group(i, u)
                    b = s % 2
                    left = NG - 1 - n if isinstance(n, int) else UNROLL
                    dve.wait_ge(kv_landed[s], 16 * TILES * (t + 1))
                    dve.wait_ge(qe_ready, n + 1)
                    qe = qe_ps[b][:, :].rearrange("p (j d) -> p j d", j=TILES)
                    nc.vector.tensor_tensor(kq[:, :, :], kv[:, s, :, 0:D], qe, ALU.mult).then_inc(kq_done, 1)
                    if not early(n, 1):
                        node = window_of(i, u, -1)
                    dve.wait_ge(eh_ready, n + 1)
                    dve.wait_ge(kq_done, n + 1)
                    eh = eh_ps[b][:, :].rearrange("p (j d) -> p j d", j=TILES)
                    nc.vector.tensor_tensor(kq[:, :, :], kq[:, :, :], eh, ALU.mult).then_inc(prod_done, 1)
                    dve.wait_ge(prod_done, n + 1)
                    by_head = kq[:, :, :].rearrange("p j (h d) -> p (j h) d", d=DH)
                    nc.vector.tensor_reduce(ssum[:, :], by_head, AX.X, ALU.add).then_inc(ssum_done, 1)
                    dve.wait_ge(ssum_done, n + 1)
                    nc.vector.tensor_scalar(sclip[:, b, :], ssum[:, :], -5.0, 5.0, ALU.max, ALU.min).then_inc(clip_done, 1)
                    if not early(n, 1):
                        add_window(i, u, -1, node)
                    if left >= 3:
                        one_hot(i, u, 3)
                    dve.wait_ge(exp_done, n + 1)
                    weigh(s, msg_done)

            dve.wait_ge(tab_copied, 2 * RT)
            for u in range(2):
                one_hot(0, u, 0)
            dve.wait_ge(inside_sum, 1)
            nc.vector.tensor_reduce(inside_all[:, :], agg_ps[0:1, 0:RT], AX.X, ALU.add).then_inc(stray_step, 1)
            dve.wait_ge(stray_step, 1)
            nc.vector.tensor_scalar(stray_i[:, :], inside_all[:, :], -1.0, float(E), ALU.mult, ALU.add).then_inc(stray_known, 1)
            dve.wait_ge(sco_clear, CHUNKS // 2)
            dve.wait_ge(msg_clear, CHUNKS // 2)
            dve.wait_ge(base_landed, 32)
            one_hot(0, 2, 0)
            edge_turn(0)
            with dve.Fori(1, TURNS - 1) as i:
                edge_turn(i)
            edge_turn(TURNS - 1)
            add_window(TURNS - 1, UNROLL - 1, 0, window_of(TURNS - 1, UNROLL - 1, 0))

            def stray_sums(g, last):
                STEPS = 8
                done = g * STEPS
                dve.wait_ge(st_gathered, 16 * 2 * TILES * (g + 1))
                dve.wait_ge(st_products, g + 1)
                nc.vector.tensor_tensor(kq[:, :, :], kv[:, 0, :, 0:D], qe_ps[0][:, :].rearrange("p (j d) -> p j d", j=TILES), ALU.mult).then_inc(st_step, 1)
                dve.wait_ge(st_step, done + 1)
                nc.vector.tensor_tensor(kq[:, :, :], kq[:, :, :], eh_ps[0][:, :].rearrange("p (j d) -> p j d", j=TILES), ALU.mult).then_inc(st_step, 1)
                dve.wait_ge(st_step, done + 2)
                nc.vector.tensor_reduce(ssum[:, :], kq[:, :, :].rearrange("p j (h d) -> p (j h) d", d=DH), AX.X, ALU.add).then_inc(st_step, 1)
                dve.wait_ge(st_step, done + 3)
                nc.vector.tensor_scalar(sclip[:, 1, :], ssum[:, :], -5.0, 5.0, ALU.max, ALU.min).then_inc(st_clip, 1)
                rel = rel_t[:, ds(g, 1), :].rearrange("p a j -> p (a j)")
                nc.vector.tensor_scalar(st_low, rel, 0.0, None, ALU.is_ge).then_inc(st_step, 1)
                dve.wait_ge(st_step, done + 4)
                nc.vector.scalar_tensor_tensor(out=st_in, in0=rel, scalar=float(WIN), in1=st_low, op0=ALU.is_lt, op1=ALU.mult).then_inc(st_step, 1)
                nc.vector.tensor_scalar(st_key_hi, st_ends[:, 1, :], 1.0, None, ALU.add).then_inc(st_step, 1)
                dve.wait_ge(st_step, done + 6)
                nc.vector.tensor_scalar(st_low, st_in, -1.0, 1.0, ALU.mult, ALU.add).then_inc(st_step, 1)
                dve.wait_ge(st_step, done + 7)
                nc.vector.tensor_tensor(st_in, st_key_hi, st_low, ALU.mult).then_inc(st_step, 1)
                dve.wait_ge(st_step, done + 8)
                if last:
                    nc.vector.memset(st_in[0:OLD // TILES, :], 0.0).then_inc(st_step, 1)
                    dve.wait_ge(st_step, done + 9)
                KEYS = 2 * (SWEEP + 1)
                nc.vector.tensor_scalar(st_key, st_in, -1.0, None, ALU.add).then_inc(st_keyed, 1)
                nc.vector.tensor_scalar(st_key_hi, st_in, -1.0 - HALF, None, ALU.add).then_inc(st_keyed, 1)
                dve.wait_ge(st_exp, g + 1)
                weigh(0, st_keyed)

                def sweep(v):
                    n = g * SWEEP + v
                    dve.wait_ge(st_keyed, g * (KEYS + 1) + 2 * v + 3)
                    places = iota[:, 0:HALF].unsqueeze(1).to_broadcast([P, TILES, HALF])
                    for half, key in enumerate((st_key, st_key_hi)):
                        op = nc.vector.tensor_tensor(st_onehot[:, :, half * HALF:(half + 1) * HALF], places,
                                                     key.unsqueeze(2).to_broadcast([P, TILES, HALF]), ALU.is_equal)
                    op.then_inc(st_onehots, 1)
                    dve.wait_ge(st_summed, n + 1)
                    for sums, part in ((acc, st_agg_ps[0]), (z_sum, st_agg_ps[1][0:HEADS])):
                        nodes = sums[:, ds(v * 2 * HALF, 2 * HALF)]
                        op = nc.vector.tensor_tensor(nodes, nodes, part[:, 0:2 * HALF], ALU.add)
                    op.then_inc(st_added, 1)
                    dve.wait_ge(st_added, n + 1)
                    for key in (st_key, st_key_hi):
                        nc.vector.tensor_scalar(key, key, -2.0 * HALF, None, ALU.add).then_inc(st_keyed, 1)

                with dve.Fori(0, SWEEP) as v:
                    sweep(v)
                dve.sem_inc(st_begun, 1)

            dve.wait_ge(agg_added, NG)
            dve.sem_inc(st_begun, 1)
            strays(dve, stray_sums)

            def z_reciprocal(k, b):
                dve.wait_ge(z_turned, k + 1)
                if not early(k, 2):
                    dve.wait_ge(zw_done, k - 1)
                nc.vector.reciprocal(z_rec[0:HQ, b, :], zT_ps[b][0:HQ, 0:TILES * HEADS]).then_inc(zr_done, 1)

            def attend(k, b, n0):
                dve.wait_ge(rT_turned, k + 1)
                m = acc[:, ds(n0, HC)]
                nc.vector.tensor_tensor(m, m, rT_ps[b][:, 0:HC], ALU.mult).then_inc(att_done, 1)

            def measure(k, n0):
                dve.wait_ge(h_done, k + 1)
                nc.vector.bn_stats(hstat[:, ds(k, 1), :].rearrange("p a s -> p (a s)"), acc[:, ds(n0, HC)]).then_inc(hstat_done, 1)

            def attend_step(k, b):
                if not (isinstance(k, int) and k >= HN):
                    z_reciprocal(k, b)
                if not early(k, 2) and not (isinstance(k, int) and k - 2 >= HN):
                    attend(k - 2, b, (k - 2) * HC)
                if not early(k, 4):
                    measure(k - 4, (k - 4) * HC)

            for k in range(4):
                attend_step(k, k % 2)
            with dve.Fori(2, HN // 2) as i:
                for b in range(2):
                    attend_step(i * 2 + b, b)
            for k in range(HN - 1, HN + 4):
                attend_step(k, k % 2)
            dve.wait_ge(hstat_done, HN)
            nc.vector.bn_aggr(bn[:, 0:2], hstat[:, :, :].rearrange("p k s -> p (k s)")).then_inc(bn_step, 1)
            dve.wait_ge(bn_std, 1)
            nc.vector.reciprocal(bn[:, 3:4], bn[:, 2:3]).then_inc(bn_step, 1)
            dve.wait_ge(bn_step, 2)
            nc.vector.tensor_tensor(bn[:, 4:5], bn[:, 3:4], gam[:, :], ALU.mult).then_inc(bn_step, 1)
            dve.wait_ge(bn_step, 3)
            nc.vector.tensor_tensor(bn[:, 5:6], bn[:, 0:1], bn[:, 4:5], ALU.mult).then_inc(bn_step, 1)
            dve.wait_ge(bn_step, 4)
            nc.vector.tensor_tensor(bn[:, 6:7], bet[:, :], bn[:, 5:6], ALU.subtract).then_inc(bn_step, 1)
            dve.wait_ge(bn_step, 5)

            def norm_nodes(c, b, n0):
                if not early(c, 2):
                    dve.wait_ge(y_done, c - 1)
                nc.vector.tensor_scalar(eaT[:, b, :], acc[:, ds(n0, NB)], bn[:, 4:5], bn[:, 6:7], ALU.mult, ALU.add).then_inc(y1_done, 1)

            def y_stats(c, s):
                dve.wait_ge(yT_ready, c + 1)
                for j in range(TILES):
                    last = nc.vector.bn_stats(ystat[:, s, j, :], yT_ps[s][:, j * P:(j + 1) * P])
                last.then_inc(ystat_done, 1)

            def y_aggregate(c, s):
                dve.wait_ge(ystat_done, c + 1)
                dve.sem_inc(aggr_begun, 1)
                for j in range(TILES):
                    last = nc.vector.bn_aggr(ymv[:, s, j, :], ystat[:, s, j, :])
                last.then_inc(yaggr_done, 1)

            def y_reciprocal(c, s):
                dve.wait_ge(ystd_done, c + 1)
                nc.vector.reciprocal(yrec[:, s, :], ystd[:, s, :]).then_inc(yrec_done, 1)

            def y_shift(c, s):
                dve.wait_ge(yrec_done, c + 1)
                nc.vector.scalar_tensor_tensor(out=ymr[:, s, :], in0=ymv[:, s, :, 0:1].rearrange("p j a -> p (j a)"), scalar=-1.0,
                                               in1=yrec[:, s, :], op0=ALU.mult, op1=ALU.mult).then_inc(ynorm_known, 1)

            def norm_step(i, u, ahead0=None, ahead=True):
                _, s, c = group(i, u)
                _, s1, c1 = group(i, u, -1)
                y_stats(c, s)
                if not early(c, 1):
                    y_reciprocal(c1, s1)
                if ahead:
                    norm_nodes(c + 2, s % 2, (c + 2) * NB if ahead0 is None else ahead0)
                y_aggregate(c, s)
                if not early(c, 1):
                    y_shift(c1, s1)

            norm_nodes(0, 0, 0)
            norm_nodes(1, 1, NB)
            for u in range(UNROLL):
                norm_step(0, u)
            with dve.Fori(1, NTURNS - 1) as i:
                for u in range(UNROLL):
                    norm_step(i, u)
            for u in range(UNROLL):
                norm_step(NTURNS - 1, u, NLAST if u == 2 else None, ahead=u < 3)
            norm_step(NTURNS, 0, ahead=False)
            y_reciprocal(CHUNKS, 0)
            y_shift(CHUNKS, 0)


_INS = ["x", "src", "dst", "edge_attr_128", "L0_gnn_WQ", "L0_gnn_WK", "L0_gnn_WV", "L0_gnn_WE", "L0_gnn_bn_gamma", "L0_gnn_bn_beta"]


def kernel(**inputs):
    import numpy as np
    import concourse.bacc as bacc
    from concourse import mybir
    from concourse.bass_utils import run_bass_kernel_spmd

    nc = bacc.Bacc("TRN2", target_bir_lowering=False, num_devices=1)
    arrays, args = {}, []
    for name in _INS:
        a = np.ascontiguousarray(inputs[name])
        arrays[f"in_{name}"] = a
        args.append(nc.dram_tensor(f"in_{name}", a.shape, mybir.dt.from_np(a.dtype), kind="ExternalInput").ap())
    x = arrays["in_x"]
    args.append(nc.dram_tensor("out", x.shape, mybir.dt.from_np(x.dtype), kind="ExternalOutput").ap())
    build(nc, *args)
    result = run_bass_kernel_spmd(nc, [arrays], core_ids=[0])
    return result.results[0]["out"]
```

```python
P = 128
HEADS = 8
TILES = 4
EG = P * TILES
WIN = 64
UNROLL = 4
NB = 512
HALF = 128
BN_EPS = 1e-5
ATTN_EPS = 1e-6
LN_EPS = 1e-5


def build(nc, x, src, dst, edge_attr, wq, wk, wv, we, gamma, beta, out):
    from contextlib import ExitStack

    import concourse.bass as bass
    from concourse import mybir

    F32, I32, BF16 = mybir.dt.float32, mybir.dt.int32, mybir.dt.bfloat16
    ALU = mybir.AluOpType
    ACT = mybir.ActivationFunctionType
    AX = mybir.AxisListType
    ds = bass.ds

    N, D = x.shape
    E = src.shape[0]
    DH = D // HEADS
    KV = 2 * D
    WHOLE = E // EG
    TAIL = E - WHOLE * EG
    NG = WHOLE + 1
    TURNS = NG // UNROLL
    LAST0 = E - EG
    OLD = EG - TAIL
    NPAD = N + WIN
    assert D == P and NG % UNROLL == 0 and 0 < TAIL < EG and OLD % TILES == 0
    RT = 4
    ROWS = NG // RT
    MASK0 = (ROWS - 1) // 32 * 32
    assert ROWS * RT == NG and ROWS <= P
    CHUNKS = N // NB
    NTURNS = CHUNKS // UNROLL
    NLAST = CHUNKS * NB
    PLAST = (N - NLAST) // TILES
    assert CHUNKS % UNROLL == 0 and PLAST * TILES == N - NLAST > 0
    EARLY = 2 * UNROLL
    CLEAR = NPAD // (CHUNKS // 2)
    assert CLEAR * (CHUNKS // 2) == NPAD
    CLEAR_M = (NPAD - 2 * RT * EG) // (CHUNKS - EARLY)
    LATE = NPAD - CLEAR_M * (CHUNKS - EARLY)
    HC = 500
    HQ = HC // TILES
    HN = N // HC
    assert HN * HC == N and HN % 2 == 1 and HQ <= P
    SWEEP = -(-N // (2 * HALF))
    assert SWEEP * 2 * HALF <= NPAD

    with ExitStack() as ctx:
        def sb(name, shape, dt=F32):
            return ctx.enter_context(nc.sbuf_tensor(name, shape, dt))

        def bank(name):
            return ctx.enter_context(nc.psum_tensor(name, [P, 512], F32))

        def sem(name):
            return ctx.enter_context(nc.semaphore(name))

        kv_rows = nc.dram_tensor("kv_rows", (N, KV), F32).ap()

        eaT_ps = bank("eaT_ps")
        ohT_ps = bank("ohT_ps")
        qw_ps = bank("qw_ps")
        agg_ps = bank("agg_ps")
        qe_ps = [bank(f"qe_ps{b}") for b in range(2)]
        eh_ps = [bank(f"eh_ps{b}") for b in range(2)]
        ohT_b = ohT_ps[:, :].bitcast(BF16)[0:WIN, 0:EG]
        tab_ps = [agg_ps, qw_ps]
        xT_ps = [eaT_ps, ohT_ps]
        proj_ps = [qe_ps, eh_ps]
        st_xT_ps, st_agg_ps = ohT_ps, [agg_ps, qw_ps]
        zT_ps, rT_ps = [eaT_ps, ohT_ps], qe_ps
        yT_ps = eh_ps + [qw_ps, agg_ps]

        xT = sb("xT", [P, NPAD])
        acc = sb("acc", [P, NPAD])
        z_sum = sb("z_sum", [HEADS, NPAD])
        src_t = sb("src_t", [P, NG, TILES])
        rel_t = sb("rel_t", [P, NG, TILES])
        ident = sb("ident", [P, P])
        ident_b = sb("ident_b", [P, P], BF16)
        ones = sb("ones", [P, 1])
        iota = sb("iota", [P, HALF])
        w_kv = sb("w_kv", [P, KV])
        w_q = sb("w_q", [P, D])
        we_sb = sb("we_sb", [P, D])
        gam = sb("gam", [P, 1])
        bet = sb("bet", [P, 1])
        eps_attn = sb("eps_attn", [P, 1])
        eps_bn = sb("eps_bn", [P, 1])
        eps_ln = sb("eps_ln", [P, 1])
        zero_col = sb("zero_col", [P, 1])
        inside = sb("inside", [P, RT])
        inside_all = sb("inside_all", [1, 1])
        stray_i = sb("stray_i", [1, 1], I32)

        def table(k, dt=F32):
            v = acc[:, k * RT * EG:(k + 1) * RT * EG]
            v = v if dt == F32 else v.bitcast(dt)
            return v.rearrange("p (r e) -> p r e", r=RT)

        rel_f, src_f = table(0), table(1)
        dst_i, src_i = table(2, I32), table(3, I32)
        dst_f, low_f = table(4), table(5)
        assert 6 * RT * EG <= NPAD
        first_i = sb("first_i", [P, RT], I32)
        first_f = sb("first_f", [P, RT])

        ea = sb("ea", [P, UNROLL, TILES, D])
        eaT = sb("eaT", [P, 2, EG])
        xw = sb("xw", [P, 2, WIN])
        node_room = sb("node_room", [P, 2, EG])
        ohT = node_room[0:WIN]
        base_i = node_room[WIN:WIN + 1, 0, 0:NG].bitcast(I32)
        qwin = sb("qwin", [WIN, 2, D])
        idx = sb("idx", [P, UNROLL, TILES], I32)
        kv = sb("kv", [P, UNROLL, TILES, KV])
        kq = sb("kq", [P, TILES, D])
        ssum = sb("ssum", [P, TILES * HEADS])
        sclip = sb("sclip", [P, 2, TILES * HEADS])
        score = sb("score", [P, TILES * HEADS])
        onehot_b = sb("onehot_b", [P, 2, TILES, WIN], BF16)
        onehot = sb("onehot", [P, UNROLL, TILES, WIN])
        x_in = ea
        kv_flat = kv[:, :, :, :].rearrange("p u j d -> p (u j d)")
        o_rows = kv_flat[:, 0:UNROLL * TILES * D].rearrange("p (s j d) -> p s j d", s=UNROLL, j=TILES)
        iota_i = kq[:, :, :].rearrange("p j d -> p (j d)")[:, 0:HALF].bitcast(I32)

        bn = sb("bn", [P, 8])
        stats = onehot[:, :, :, :].rearrange("p b j n -> p (b j n)")
        hstat = stats[:, 0:HN * 6].rearrange("p (k s) -> p k s", s=6)
        ystat = stats[:, HN * 6:(HN + UNROLL * TILES) * 6].rearrange("p (s j a) -> p s j a", s=UNROLL, a=6)
        ymv = sb("ymv", [P, UNROLL, TILES, 2])
        ystd = sb("ystd", [P, UNROLL, TILES])
        yrec = sb("yrec", [P, UNROLL, TILES])
        ymr = sb("ymr", [P, UNROLL, TILES])
        y_sum = ea[:, :, :, :].rearrange("p s j d -> p s (j d)")
        z_rec = sclip
        z_wide = [room.rearrange("p (q d) -> p q d", d=DH) for room in
                  (kq[:, :, :].rearrange("p j d -> p (j d)"), kv_flat[:, 0:EG])]

        consts_made = sem("consts_made")
        consts_cast = sem("consts_cast")
        ident_zero = sem("ident_zero")
        tail_masked = sem("tail_masked")
        xT_padded = sem("xT_padded")
        wkv_landed = sem("wkv_landed")
        w_landed = sem("w_landed")
        wq_scaled = sem("wq_scaled")
        dst_landed = sem("dst_landed")
        src_landed = sem("src_landed")
        first_landed = sem("first_landed")
        base_landed = sem("base_landed")
        first_cast = sem("first_cast")
        dst_cast = sem("dst_cast")
        src_cast = sem("src_cast")
        rel_done = sem("rel_done")
        low_done = sem("low_done")
        inside_done = sem("inside_done")
        tab_turned = sem("tab_turned")
        tab_copied = sem("tab_copied")
        inside_sum = sem("inside_sum")
        stray_step = sem("stray_step")
        stray_known = sem("stray_known")
        msg_clear = sem("msg_clear")
        sco_clear = sem("sco_clear")

        x_landed = [sem(f"x_landed{s}") for s in range(UNROLL)]
        kv_stored = [sem(f"kv_stored{s}") for s in range(UNROLL)]
        xT_turned = sem("xT_turned")
        xT_copied = sem("xT_copied")
        xT_kept = sem("xT_kept")
        proj_ready = sem("proj_ready")
        proj_copied = sem("proj_copied")

        ea_landed = [sem(f"ea_landed{u}") for u in range(UNROLL)]
        kv_landed = [sem(f"kv_landed{u}") for u in range(UNROLL)]
        idx_ready = sem("idx_ready")
        gather_begun = sem("gather_begun")
        eaT_ready = sem("eaT_ready")
        eaT_copied = sem("eaT_copied")
        ohT_ready = sem("ohT_ready")
        ohT_copied = sem("ohT_copied")
        xw_ready = sem("xw_ready")
        qw_ready = sem("qw_ready")
        qw_copied = sem("qw_copied")
        qe_ready = sem("qe_ready")
        eh_ready = sem("eh_ready")
        kq_done = sem("kq_done")
        prod_done = sem("prod_done")
        ssum_done = sem("ssum_done")
        clip_done = sem("clip_done")
        exp_done = sem("exp_done")
        onehot_done = sem("onehot_done")
        onehot_cast = sem("onehot_cast")
        msg_done = sem("msg_done")
        agg_ready = sem("agg_ready")
        agg_added = sem("agg_added")

        st_ends = idx
        st_x = kv[:, 1, :, 0:D]
        st_onehot = kv[:, 2]
        st_low = sclip[:, 0, 0:TILES]
        st_in = sclip[:, 0, TILES:2 * TILES]
        st_key = sclip[:, 0, 2 * TILES:3 * TILES]
        st_key_hi = sclip[:, 0, 3 * TILES:4 * TILES]
        st_begun = sem("st_begun")
        st_loaded = sem("st_loaded")
        st_gathering = sem("st_gathering")
        st_gathered = sem("st_gathered")
        st_turned = sem("st_turned")
        st_copied = sem("st_copied")
        st_products = sem("st_products")
        st_step = sem("st_step")
        st_clip = sem("st_clip")
        st_exp = sem("st_exp")
        st_keyed = sem("st_keyed")
        st_onehots = sem("st_onehots")
        st_summed = sem("st_summed")
        st_added = sem("st_added")

        def strays(eng, group_body):
            eng.wait_ge(stray_known, 1)
            count = eng.value_load(stray_i[0:1, 0:1], min_val=0, max_val=E)
            with eng.If(count > 0):
                with eng.Fori(0, NG - 1) as g:
                    group_body(g, False)
                group_body(NG - 1, True)

        z_ready = sem("z_ready")
        z_turning = sem("z_turning")
        z_turned = sem("z_turned")
        zr_done = sem("zr_done")
        zw_done = sem("zw_done")
        rT_turned = sem("rT_turned")
        att_done = sem("att_done")
        h_done = sem("h_done")
        hstat_done = sem("hstat_done")
        bn_step = sem("bn_step")
        bn_std = sem("bn_std")
        y1_done = sem("y1_done")
        y_done = sem("y_done")
        yT_ready = sem("yT_ready")
        ystat_done = sem("ystat_done")
        aggr_begun = sem("aggr_begun")
        yaggr_done = sem("yaggr_done")
        ystd_done = sem("ystd_done")
        yrec_done = sem("yrec_done")
        ynorm_known = sem("ynorm_known")
        o_done = sem("o_done")
        out_stored = [sem(f"out_stored{s}") for s in range(UNROLL)]

        def group(i, u, k=0):
            t, s = i + (u + k) // UNROLL, (u + k) % UNROLL
            return t, s, t * UNROLL + s

        def early(n, count):
            return isinstance(n, int) and n < count

        def node_rows(rows, n0, parts=P):
            return rows[ds(n0, parts * TILES), :].rearrange("(p j) d -> p j d", j=TILES)

        def tiled(room, parts=P):
            return room.rearrange("p (j n) -> p j n", j=TILES)[:, :, 0:parts]

        block = ctx.enter_context(nc.Block())

        @block.sync
        def _(sp):
            def load_x(c, s, n0, parts=P):
                if not early(c, UNROLL):
                    sp.wait_ge(xT_turned, c - UNROLL + 1)
                sp.dma_start(x_in[0:parts, s], node_rows(x, n0, parts)).then_inc(x_landed[s], 16)

            def store_rows(c, s, n0, parts=P):
                sp.wait_ge(proj_copied, 2 * (c + 1))
                sp.dma_start(node_rows(kv_rows, n0, parts), kv[0:parts, s]).then_inc(kv_stored[s], 16)

            def load_ends(ends, table_i, landed, tail0, tail_to):
                full = (RT - 1) * ROWS * EG
                sp.dma_start(table_i[0:ROWS, 0:RT - 1, :], ends[0:full].rearrange("(r p e) -> p r e", p=ROWS, e=EG)).then_inc(landed, 16)
                sp.dma_start(table_i[0:ROWS - 1, RT - 1, :], ends[full:WHOLE * EG].rearrange("(p e) -> p e", e=EG)).then_inc(landed, 16)
                sp.dma_start(table_i[ROWS - 1:ROWS, RT - 1, tail_to:EG], ends[tail0:E].rearrange("(a e) -> a e", a=1)).then_inc(landed, 16)

            load_x(0, 0, 0)
            for k, w in enumerate((wk, wv)):
                sp.dma_start(w_kv[:, k * D:(k + 1) * D], w).then_inc(wkv_landed, 16)
            load_x(1, 1, NB)
            load_x(2, 2, 2 * NB)
            load_x(3, 3, 3 * NB)
            with nc.allow_non_contiguous_dma(reason="one word of each group"):
                words = dst[0:WHOLE * EG].rearrange("(g e) -> g e", e=EG)[:, 0:1]
                full = (RT - 1) * ROWS
                sp.dma_start(first_i[0:ROWS, 0:RT - 1], words[0:full, :].rearrange("(r p) a -> p (r a)", p=ROWS)).then_inc(first_landed, 16)
                sp.dma_start(first_i[0:ROWS - 1, RT - 1:RT], words[full:WHOLE, :]).then_inc(first_landed, 16)
                sp.dma_start(first_i[ROWS - 1:ROWS, RT - 1:RT], dst[E - TAIL:E - TAIL + 1].rearrange("(a b) -> a b", a=1)).then_inc(first_landed, 16)
                sp.wait_ge(tail_masked, 1)
                load_ends(dst, dst_i, dst_landed, E - TAIL, OLD)
                load_ends(src, src_i, src_landed, LAST0, 0)

            def chunk_turn(i):
                for u in range(UNROLL):
                    c = i * UNROLL + u
                    load_x(c + UNROLL, u, (c + UNROLL) * NB)
                    store_rows(c, u, c * NB)

            chunk_turn(0)
            sp.dma_start(w_q[:, :], wq).then_inc(w_landed, 16)
            sp.dma_start(we_sb[:, :], we).then_inc(w_landed, 16)
            sp.dma_start(gam[:, :], gamma.rearrange("(d a) -> d a", a=1)).then_inc(w_landed, 16)
            sp.dma_start(bet[:, :], beta.rearrange("(d a) -> d a", a=1)).then_inc(w_landed, 16)
            with nc.allow_non_contiguous_dma(reason="one word of each group"):
                sp.dma_start(base_i[0:1, 0:WHOLE].rearrange("a (g b) -> a g b", b=1), words.rearrange("(a g) b -> a g b", a=1)).then_inc(base_landed, 16)
                sp.dma_start(base_i[0:1, WHOLE:NG], dst[E - TAIL:E - TAIL + 1].rearrange("(a b) -> a b", a=1)).then_inc(base_landed, 16)
            with sp.Fori(1, NTURNS - 1) as i:
                chunk_turn(i)
            load_x(CHUNKS, 0, NLAST, PLAST)
            for u in range(UNROLL):
                c = CHUNKS - UNROLL + u
                store_rows(c, u, c * NB)
            store_rows(CHUNKS, 0, NLAST, PLAST)

            def edge_loads(i, last=False):
                for u in range(UNROLL):
                    _, s, n = group(i, u)
                    e0 = LAST0 if last and u == UNROLL - 1 else n * EG
                    if not early(n, UNROLL):
                        sp.wait_ge(eaT_ready, n - UNROLL + 1)
                    part = edge_attr[ds(e0, EG), :].rearrange("(p j) d -> p j d", j=TILES)
                    sp.dma_start(ea[:, s], part).then_inc(ea_landed[s], 16)

            sp.wait_ge(xT_turned, CHUNKS + 1)
            edge_loads(0)
            with sp.Fori(1, TURNS - 1) as i:
                edge_loads(i)
            edge_loads(TURNS - 1, last=True)

            def stray_loads(g, last):
                sp.wait_ge(st_begun, g + 1)
                e0 = LAST0 if last else g * EG
                sp.dma_start(ea[:, 0], edge_attr[ds(e0, EG), :].rearrange("(p j) d -> p j d", j=TILES)).then_inc(st_loaded, 16)
                for k, ends in enumerate((src, dst)):
                    sp.dma_start(st_ends[:, k, :], ends[ds(e0, EG)].rearrange("(p j) -> p j", j=TILES)).then_inc(st_loaded, 16)

            strays(sp, stray_loads)

            def store_out(c, s, n0, parts=P):
                sp.wait_ge(o_done, c + 1)
                sp.dma_start(node_rows(out, n0, parts), o_rows[0:parts, s]).then_inc(out_stored[s], 16)

            with sp.Fori(0, NTURNS) as i:
                for u in range(UNROLL):
                    store_out(i * UNROLL + u, u, (i * UNROLL + u) * NB)
            store_out(CHUNKS, 0, NLAST, PLAST)
            for s in range(UNROLL):
                sp.wait_ge(out_stored[s], 16 * (NTURNS + (s == 0)))

        @block.gpsimd
        def _(pool):
            nc.gpsimd.memset(ident[:, :], 0.0).then_inc(ident_zero, 1)
            pool.wait_ge(ident_zero, 1)
            nc.gpsimd.affine_select(out=ident[:, :], in_=ident[:, :], compare_op=ALU.not_equal, fill=1.0, base=0,
                                    pattern=[[-1, P]], channel_multiplier=1).then_inc(consts_made, 1)
            nc.gpsimd.iota(iota_i[:, :], pattern=[[1, HALF]], base=0, channel_multiplier=0).then_inc(consts_made, 1)
            nc.gpsimd.memset(xT[:, N:NPAD], 0.0).then_inc(xT_padded, 1)

            def keep_xT(c, b, n0, parts=P):
                pool.wait_ge(xT_copied, c + 1)
                nodes = xT[:, ds(n0, parts * TILES)].rearrange("f (p j) -> f j p", j=TILES)
                nc.gpsimd.tensor_copy(nodes, tiled(eaT[:, b, :], parts)).then_inc(xT_kept, 1)

            with pool.Fori(0, CHUNKS // 2) as i:
                for b in range(2):
                    keep_xT(i * 2 + b, b, (i * 2 + b) * NB)
            keep_xT(CHUNKS, 0, NLAST, PLAST)

            for s in range(UNROLL):
                pool.wait_ge(kv_stored[s], 16 * (NTURNS + (s == 0)))

            def gathers(i):
                for u in range(UNROLL):
                    _, s, n = group(i, u)
                    pool.wait_ge(idx_ready, n + 1)
                    pool.sem_inc(gather_begun, 1)
                    for j in range(TILES):
                        pool.indirect_dma_start(
                            out=kv[:, s, j, :], out_offset=None, in_=kv_rows,
                            in_offset=bass.IndirectOffsetOnAxis(ap=idx[:, s, j:j + 1], axis=0),
                        ).then_inc(kv_landed[s], 16)

            with pool.Fori(0, TURNS) as i:
                gathers(i)

            def stray_gathers(g, last):
                pool.wait_ge(st_loaded, 48 * (g + 1))
                pool.sem_inc(st_gathering, 1)
                for j in range(TILES):
                    for rows, k, to in ((kv_rows, 0, kv[:, 0, j, :]), (x, 1, st_x[:, j, :])):
                        pool.indirect_dma_start(
                            out=to, out_offset=None, in_=rows,
                            in_offset=bass.IndirectOffsetOnAxis(ap=st_ends[:, k, j:j + 1], axis=0),
                        ).then_inc(st_gathered, 16)

            strays(pool, stray_gathers)

            def residual(k, n0):
                pool.wait_ge(att_done, k + 1)
                h = acc[:, ds(n0, HC)]
                nc.gpsimd.tensor_tensor(h, h, xT[:, ds(n0, HC)], ALU.add).then_inc(h_done, 1)

            with pool.Fori(0, HN) as k:
                residual(k, k * HC)

            def add_x(c, s, n0, parts=P):
                pool.wait_ge(y1_done, c + 1)
                if not early(c, UNROLL):
                    pool.wait_ge(yT_ready, c - UNROLL + 1)
                nodes = parts * TILES
                nc.gpsimd.tensor_tensor(y_sum[:, s, 0:nodes], eaT[:, s % 2, 0:nodes], xT[:, ds(n0, nodes)], ALU.add).then_inc(y_done, 1)

            for s in range(UNROLL):
                add_x(s, s, s * NB)
            with pool.Fori(1, NTURNS) as i:
                for u in range(UNROLL):
                    add_x(i * UNROLL + u, u, (i * UNROLL + u) * NB)
            add_x(CHUNKS, 0, NLAST, PLAST)

        @block.scalar
        def _(act):
            def proj_copy(c, s, turn, parts=P):
                if not early(turn, 1):
                    act.wait_ge(kv_stored[s], 16 * turn)
                for half in range(2):
                    act.wait_ge(proj_ready, 2 * c + half + 1)
                    rows = kv[0:parts, s, 2 * half:2 * half + 2, :].rearrange("p j d -> p (j d)")
                    nc.scalar.copy(rows, proj_ps[s % 2][half][0:parts, :]).then_inc(proj_copied, 1)

            def clear_scores(k):
                nc.scalar.copy(z_sum[:, ds(k * CLEAR, CLEAR)], zero_col[0:HEADS, :].to_broadcast([HEADS, CLEAR])).then_inc(sco_clear, 1)

            act.wait_ge(consts_cast, 1)
            clear_scores(0)
            clear_scores(1)
            for c in range(UNROLL):
                proj_copy(c, c, 0)
                if c == 2:
                    act.wait_ge(src_landed, 16 * 3)
                if c >= 2:
                    for r in (2 * c - 4, 2 * c - 3):
                        nc.scalar.copy(src_f[0:ROWS, r, :], src_i[0:ROWS, r, :]).then_inc(src_cast, 1)
            with act.Fori(1, NTURNS) as i:
                for u in range(UNROLL):
                    proj_copy(i * UNROLL + u, u, i)
                    if u % 2:
                        clear_scores(i * 2 + u // 2)
            proj_copy(CHUNKS, 0, NTURNS, PLAST)

            def window_x(i, u, k):
                _, s, n = group(i, u, k)
                node = act.value_load(base_i[0:1, ds(n, 1)], min_val=0, max_val=N - 1)
                if not early(n, 2):
                    act.wait_ge(qw_ready, n - 1)
                nc.scalar.copy(xw[:, s % 2, :], xT[:, ds(node, WIN)]).then_inc(xw_ready, 1)

            def copies(i, u, k):
                _, s, n = group(i, u, k)
                b = s % 2
                act.wait_ge(eaT_ready, n + 1)
                if not early(n, 2):
                    act.wait_ge(eh_ready, n - 1)
                nc.scalar.copy(eaT[:, b, :], eaT_ps[:, :]).then_inc(eaT_copied, 1)
                act.wait_ge(ohT_ready, n + 1)
                if not early(n, 2):
                    act.wait_ge(qe_ready, n - 1)
                nc.scalar.copy(ohT[:, b, :], ohT_b).then_inc(ohT_copied, 1)
                nc.scalar.copy(onehot[:, s], onehot_b[:, b]).then_inc(onehot_cast, 1)
                act.wait_ge(qw_ready, n + 1)
                nc.scalar.copy(qwin[:, b, :], qw_ps[0:WIN, 0:D]).then_inc(qw_copied, 1)

            def indices(i, u, k):
                _, s, n = group(i, u, k)
                nc.scalar.copy(idx[:, s, :], src_t[:, ds(n, 1), :].rearrange("p a j -> p (a j)")).then_inc(idx_ready, 1)

            def exponent(i, u):
                _, _, n = group(i, u)
                act.wait_ge(clip_done, n + 1)
                nc.scalar.activation(score[:, :], sclip[:, u % 2, :], ACT.Exp).then_inc(exp_done, 1)

            def edge_turn(i):
                for u in range(UNROLL):
                    left = NG - 1 - group(i, u)[2] if isinstance(i, int) else UNROLL
                    if not early(group(i, u)[2], 1):
                        act.wait_ge(agg_ready, group(i, u)[2])
                    if left >= 3:
                        indices(i, u, 3)
                    exponent(i, u)
                    if left >= 2:
                        copies(i, u, 2)
                    if left >= 3:
                        window_x(i, u, 3)

            act.wait_ge(tab_copied, 1)
            for u in range(3):
                indices(0, u, 0)
            act.wait_ge(base_landed, 32)
            act.wait_ge(xT_kept, CHUNKS + 1)
            act.wait_ge(xT_padded, 1)
            window_x(0, 0, 0)
            window_x(0, 1, 0)
            copies(0, 0, 0)
            copies(0, 1, 0)
            window_x(0, 2, 0)
            act.wait_ge(tab_copied, 2 * RT)
            edge_turn(0)
            with act.Fori(1, TURNS - 1) as i:
                edge_turn(i)
            edge_turn(TURNS - 1)

            def stray_activations(g, last):
                act.wait_ge(st_turned, 2 * g + 1)
                nc.scalar.copy(eaT[:, 0, :], eaT_ps[:, :]).then_inc(st_copied, 1)
                act.wait_ge(st_turned, 2 * g + 2)
                nc.scalar.copy(eaT[:, 1, :], st_xT_ps[:, :]).then_inc(st_copied, 1)
                act.wait_ge(st_clip, g + 1)
                nc.scalar.activation(score[:, :], sclip[:, 1, :], ACT.Exp).then_inc(st_exp, 1)
                act.wait_ge(st_added, (g + 1) * SWEEP)

            strays(act, stray_activations)

            def z_copy(k, b, n0):
                if not early(k, 2):
                    act.wait_ge(z_turned, k - 1)
                nc.scalar.activation(eaT[0:HEADS, b, 0:HC], z_sum[:, ds(n0, HC)], ACT.Identity, bias=eps_attn[0:HEADS, :]).then_inc(z_ready, 1)

            def z_spread(k, b):
                act.wait_ge(zr_done, k + 1)
                if not early(k, 2):
                    act.wait_ge(rT_turned, k - 1)
                wide = z_rec[0:HQ, b, :].unsqueeze(2).to_broadcast([HQ, TILES * HEADS, DH])
                nc.scalar.copy(z_wide[b][0:HQ], wide).then_inc(zw_done, 1)

            act.wait_ge(agg_added, NG)
            z_copy(0, 0, 0)
            for k in range(2):
                z_copy(k + 1, (k + 1) % 2, (k + 1) * HC)
                z_spread(k, k)
            with act.Fori(1, HN // 2) as i:
                for b in range(2):
                    k = i * 2 + b
                    z_copy(k + 1, (b + 1) % 2, (k + 1) * HC)
                    z_spread(k, b)
            z_spread(HN - 1, 0)
            act.wait_ge(bn_step, 1)
            nc.scalar.activation(bn[:, 2:3], bn[:, 1:2], ACT.Sqrt, bias=eps_bn[:, :]).then_inc(bn_std, 1)

            def y_std(c, s, parts=P):
                act.wait_ge(yaggr_done, c + 1)
                nc.scalar.activation(ystd[0:parts, s, :], ymv[0:parts, s, :, 1:2].rearrange("p j a -> p (j a)"), ACT.Sqrt, bias=eps_ln[0:parts, :]).then_inc(ystd_done, 1)

            def normalise(c, s, turn, parts=P):
                act.wait_ge(ynorm_known, c + 1)
                if not early(turn, 1):
                    act.wait_ge(out_stored[s], 16 * turn)
                for j in range(TILES):
                    last = nc.scalar.activation(o_rows[0:parts, s, j, :], yT_ps[s][0:parts, j * P:(j + 1) * P], ACT.Identity,
                                                scale=yrec[0:parts, s, j:j + 1], bias=ymr[0:parts, s, j:j + 1])
                last.then_inc(o_done, 1)

            def node_turn_out(i):
                for u in range(UNROLL):
                    y_std(i * UNROLL + u, u)
                    if not (u == 0 and early(i, 1)):
                        t, s, c = group(i, u, -1)
                        normalise(c, s, t)

            node_turn_out(0)
            with act.Fori(1, NTURNS) as i:
                node_turn_out(i)
            y_std(CHUNKS, 0, PLAST)
            normalise(CHUNKS - 1, UNROLL - 1, NTURNS - 1)
            normalise(CHUNKS, 0, NTURNS, PLAST)

        @block.tensor
        def _(pe):
            def turn_table(k):
                r = k // 2
                table_f, made = (rel_f, rel_done) if k % 2 else (src_f, src_cast)
                pe.wait_ge(made, r + 1)
                if k >= 2:
                    pe.wait_ge(tab_copied, k - 1)
                for j in range(TILES):
                    last = pe.transpose(tab_ps[k % 2][:, j * ROWS:(j + 1) * ROWS], table_f[0:ROWS, r, j::TILES], ident[0:ROWS, 0:ROWS])
                last.then_inc(tab_turned, 1)

            def turn_x(c, s, turn, parts=P):
                pe.wait_ge(x_landed[s], 16 * (turn + 1))
                if not early(c, 2):
                    pe.wait_ge(xT_copied, c - 1)
                for j in range(TILES):
                    last = pe.transpose(xT_ps[s % 2][:, j * P:j * P + parts], x_in[0:parts, s, j, :], ident[0:parts, 0:parts])
                last.then_inc(xT_turned, 1)

            def project(c, s, parts=P):
                pe.wait_ge(xT_copied, c + 1)
                for half in range(2):
                    if not early(c, 2):
                        pe.wait_ge(proj_copied, 2 * (c - 2) + half + 1)
                    for j in (2 * half, 2 * half + 1):
                        last = pe.matmul(proj_ps[s % 2][half][0:parts, (j % 2) * KV:(j % 2 + 1) * KV], eaT[:, s % 2, j * P:j * P + parts], w_kv[:, :], start=True, stop=True)
                    last.then_inc(proj_ready, 1)

            def node_turn(i, left=UNROLL):
                for u in range(UNROLL):
                    c = i * UNROLL + u
                    project(c, u)
                    t, s, ahead = group(i, u, 2)
                    if u < left:
                        turn_x(ahead, s, t, PLAST if isinstance(ahead, int) and ahead == CHUNKS else P)

            pe.wait_ge(consts_made, 1)
            turn_x(0, 0, 0)
            turn_x(1, 1, 0)
            pe.wait_ge(wkv_landed, 16 * 2)
            node_turn(0)
            with pe.Fori(1, NTURNS - 1) as i:
                node_turn(i)
            node_turn(NTURNS - 1, left=3)
            project(CHUNKS, 0, PLAST)
            for k in range(2 * RT):
                turn_table(k)
            pe.wait_ge(inside_done, RT)
            pe.wait_ge(consts_cast, 1)
            pe.wait_ge(tab_copied, 2 * RT)
            pe.matmul(agg_ps[0:1, 0:RT], ones[:, :], inside[:, :], start=True, stop=True).then_inc(inside_sum, 1)

            def turns(i, u, k):
                t, s, n = group(i, u, k)
                pe.wait_ge(ea_landed[s], 16 * (t + 1))
                pe.wait_ge(onehot_done, n + 1)
                pe.wait_ge(xw_ready, n + 1)
                if not early(n, 1):
                    pe.wait_ge(eaT_copied, n)
                    pe.wait_ge(ohT_copied, n)
                    pe.wait_ge(qw_copied, n)
                for j in range(TILES):
                    last = pe.transpose(eaT_ps[:, j * P:(j + 1) * P], ea[:, s, j, :], ident[:, :])
                last.then_inc(eaT_ready, 1)
                for j in range(TILES):
                    last = pe.transpose(ohT_b[:, j * P:(j + 1) * P], onehot_b[:, s % 2, j, :], ident_b[:, :])
                last.then_inc(ohT_ready, 1)
                pe.matmul(qw_ps[0:WIN, 0:D], xw[:, s % 2, :], w_q[:, :], start=True, stop=True).then_inc(qw_ready, 1)

            def spread_q(i, u, k):
                _, s, n = group(i, u, k)
                pe.wait_ge(ohT_copied, n + 1)
                pe.wait_ge(qw_copied, n + 1)
                if not early(n, 2):
                    pe.wait_ge(kq_done, n - 1)
                for j in range(TILES):
                    last = pe.matmul(qe_ps[s % 2][:, j * P:(j + 1) * P], ohT[:, s % 2, j * P:(j + 1) * P], qwin[:, s % 2, :], start=True, stop=True)
                last.then_inc(qe_ready, 1)

            def edge_product(i, u, k):
                _, s, n = group(i, u, k)
                pe.wait_ge(eaT_copied, n + 1)
                if not early(n, 2):
                    pe.wait_ge(prod_done, n - 1)
                for j in range(TILES):
                    last = pe.matmul(eh_ps[s % 2][:, j * P:(j + 1) * P], eaT[:, s % 2, j * P:(j + 1) * P], we_sb[:, :], start=True, stop=True)
                last.then_inc(eh_ready, 1)

            def sum_window(i, u):
                _, s, n = group(i, u)
                pe.wait_ge(onehot_cast, n + 1)
                pe.wait_ge(msg_done, n + 1)
                if not early(n, 1):
                    pe.wait_ge(agg_added, n)
                for j in range(TILES):
                    pe.matmul(agg_ps[:, 0:WIN], kv[:, s, j, D:KV], onehot[:, s, j, :], start=(j == 0), stop=(j == TILES - 1))
                for j in range(TILES):
                    last = pe.matmul(agg_ps[0:HEADS, WIN:2 * WIN], score[:, j * HEADS:(j + 1) * HEADS], onehot[:, s, j, :], start=(j == 0), stop=(j == TILES - 1))
                last.then_inc(agg_ready, 1)

            def edge_turn(i):
                for u in range(UNROLL):
                    left = NG - 1 - group(i, u)[2] if isinstance(i, int) else UNROLL
                    if left >= 2:
                        turns(i, u, 2)
                    if left >= 1:
                        spread_q(i, u, 1)
                        edge_product(i, u, 1)
                    sum_window(i, u)

            pe.wait_ge(proj_copied, 2 * (CHUNKS + 1))
            pe.wait_ge(wq_scaled, 1)
            pe.wait_ge(stray_step, 1)
            turns(0, 0, 0)
            turns(0, 1, 0)
            spread_q(0, 0, 0)
            edge_product(0, 0, 0)
            edge_turn(0)
            with pe.Fori(1, TURNS - 1) as i:
                edge_turn(i)
            edge_turn(TURNS - 1)

            def stray_products(g, last):
                pe.wait_ge(st_loaded, 48 * (g + 1))
                for j in range(TILES):
                    op = pe.transpose(eaT_ps[:, j * P:(j + 1) * P], ea[:, 0, j, :], ident[:, :])
                op.then_inc(st_turned, 1)
                pe.wait_ge(st_gathered, 16 * 2 * TILES * (g + 1))
                for j in range(TILES):
                    op = pe.transpose(st_xT_ps[:, j * P:(j + 1) * P], st_x[:, j, :], ident[:, :])
                op.then_inc(st_turned, 1)
                pe.wait_ge(st_copied, 2 * g + 2)
                for j in range(TILES):
                    pe.matmul(eh_ps[0][:, j * P:(j + 1) * P], eaT[:, 0, j * P:(j + 1) * P], we_sb[:, :], start=True, stop=True)
                for j in range(TILES):
                    op = pe.matmul(qe_ps[0][:, j * P:(j + 1) * P], eaT[:, 1, j * P:(j + 1) * P], w_q[:, :], start=True, stop=True)
                op.then_inc(st_products, 1)

                def sweep(v):
                    pe.wait_ge(st_onehots, g * SWEEP + v + 1)
                    for j in range(TILES):
                        pe.matmul(st_agg_ps[0][:, 0:2 * HALF], kv[:, 0, j, D:KV], st_onehot[:, j, :], start=(j == 0), stop=(j == TILES - 1))
                    for j in range(TILES):
                        op = pe.matmul(st_agg_ps[1][0:HEADS, 0:2 * HALF], score[:, j * HEADS:(j + 1) * HEADS], st_onehot[:, j, :], start=(j == 0), stop=(j == TILES - 1))
                    op.then_inc(st_summed, 1)

                with pe.Fori(0, SWEEP) as v:
                    sweep(v)

            strays(pe, stray_products)

            def turn_z(k, b):
                pe.wait_ge(z_ready, k + 1)
                if not early(k, 2):
                    pe.wait_ge(zr_done, k - 1)
                pe.sem_inc(z_turning, 1)
                for j in range(TILES):
                    last = pe.transpose(zT_ps[b][0:HQ, j * HEADS:(j + 1) * HEADS], eaT[0:HEADS, b, j * HQ:(j + 1) * HQ], ident[0:HEADS, 0:HEADS])
                last.then_inc(z_turned, 1)

            def turn_back(k, b):
                pe.wait_ge(zw_done, k + 1)
                if not early(k, 2):
                    pe.wait_ge(att_done, k - 1)
                for j in range(TILES):
                    quarter = z_wide[b][0:HQ, j * HEADS:(j + 1) * HEADS, :].rearrange("p h d -> p (h d)")
                    last = pe.transpose(rT_ps[b][:, j * HQ:(j + 1) * HQ], quarter, ident[0:HQ, 0:HQ])
                last.then_inc(rT_turned, 1)

            turn_z(0, 0)
            for k in range(2):
                turn_z(k + 1, (k + 1) % 2)
                turn_back(k, k)
            with pe.Fori(1, HN // 2) as i:
                for b in range(2):
                    turn_z(i * 2 + b + 1, (b + 1) % 2)
                    turn_back(i * 2 + b, b)
            turn_back(HN - 1, 0)

            def turn_y(c, s, parts=P):
                pe.wait_ge(y_done, c + 1)
                if not early(c, UNROLL):
                    pe.wait_ge(o_done, c - UNROLL + 1)
                for j in range(TILES):
                    last = pe.transpose(yT_ps[s][0:parts, j * P:(j + 1) * P], y_sum[:, s, j:parts * TILES:TILES], ident[:, :])
                last.then_inc(yT_ready, 1)

            for s in range(UNROLL):
                turn_y(s, s)
            with pe.Fori(1, NTURNS) as i:
                for u in range(UNROLL):
                    turn_y(i * UNROLL + u, u)
            turn_y(CHUNKS, 0, PLAST)

        @block.vector
        def _(dve):
            nc.vector.memset(dst_i[MASK0:ROWS, RT - 1, :], -(1 << 20)).then_inc(tail_masked, 1)
            nc.vector.memset(zero_col[:, :], 0.0)
            nc.vector.memset(ones[:, :], 1.0)
            nc.vector.memset(eps_attn[:, :], ATTN_EPS)
            nc.vector.memset(eps_bn[:, :], BN_EPS)
            nc.vector.memset(eps_ln[:, :], LN_EPS)
            nc.vector.memset(inside[:, :], 0.0)
            dve.wait_ge(consts_made, 2)
            nc.vector.tensor_copy(ident_b[:, :], ident[:, :])
            nc.vector.tensor_copy(iota[:, :], iota_i[:, :]).then_inc(consts_cast, 1)

            def xT_copy(c, b, parts=P):
                dve.wait_ge(xT_turned, c + 1)
                if not early(c, 2):
                    dve.wait_ge(proj_ready, 2 * (c - 1))
                    dve.wait_ge(xT_kept, c - 1)
                nc.vector.tensor_copy(tiled(eaT[:, b, :], parts), tiled(xT_ps[b][:, :], parts)).then_inc(xT_copied, 1)

            def relative(r):
                dve.wait_ge(dst_cast, r + 1)
                rel = rel_f[0:ROWS, r, :]
                nc.vector.tensor_scalar(rel, dst_f[0:ROWS, r, :], first_f[0:ROWS, r:r + 1], None, ALU.subtract).then_inc(rel_done, 1)
                dve.wait_ge(rel_done, r + 1)
                nc.vector.tensor_scalar(low_f[0:ROWS, r, :], rel, 0.0, None, ALU.is_ge).then_inc(low_done, 1)
                dve.wait_ge(low_done, r + 1)
                nc.vector.scalar_tensor_tensor(out=dst_f[0:ROWS, r, :], in0=rel, scalar=float(WIN), in1=low_f[0:ROWS, r, :],
                                               op0=ALU.is_lt, op1=ALU.mult, accum_out=inside[0:ROWS, r:r + 1]).then_inc(inside_done, 1)

            def table_copy(k):
                g0 = k // 2 * ROWS
                dve.wait_ge(tab_turned, k + 1)
                tab = (rel_t if k % 2 else src_t)[:, g0:g0 + ROWS, :].rearrange("p g j -> p j g")
                nc.vector.tensor_copy(tab, tab_ps[k % 2][:, 0:TILES * ROWS].rearrange("p (j g) -> p j g", j=TILES)).then_inc(tab_copied, 1)

            xT_copy(0, 0)
            xT_copy(1, 1)
            dve.wait_ge(first_landed, 16 * 3)
            nc.vector.tensor_copy(first_f[0:ROWS, :], first_i[0:ROWS, :]).then_inc(first_cast, 1)
            dve.wait_ge(dst_landed, 16 * 3)
            for r in range(RT):
                nc.vector.tensor_copy(dst_f[0:ROWS, r, :], dst_i[0:ROWS, r, :]).then_inc(dst_cast, 1)
                if r % 2:
                    xT_copy(2 + r // 2, r // 2)
            dve.wait_ge(first_cast, 1)
            for r in range(RT):
                relative(r)
                xT_copy(EARLY - RT + r, r % 2)
            dve.wait_ge(src_cast, RT)
            dve.wait_ge(inside_done, RT)
            with dve.Fori(EARLY // 2, CHUNKS // 2) as i:
                for b in range(2):
                    c = i * 2 + b
                    xT_copy(c, b)
                    piece = acc[:, ds((c - EARLY) * CLEAR_M + LATE, CLEAR_M)]
                    nc.vector.tensor_copy(piece, zero_col[:, :].to_broadcast([P, CLEAR_M])).then_inc(msg_clear, 1)
            xT_copy(CHUNKS, 0, PLAST)
            for k in range(2 * RT):
                table_copy(k)
            dve.wait_ge(w_landed, 16 * 4)
            nc.vector.tensor_scalar(w_q[:, :], w_q[:, :], DH ** -0.5, None, ALU.mult).then_inc(wq_scaled, 1)

            def one_hot(i, u, k):
                _, s, n = group(i, u, k)
                if not early(n, 2):
                    dve.wait_ge(onehot_cast, n - 1)
                places = iota[:, 0:WIN].unsqueeze(1).to_broadcast([P, TILES, WIN])
                rel = rel_t[:, ds(n, 1), :].rearrange("p a j -> p (a j)").unsqueeze(2).to_broadcast([P, TILES, WIN])
                nc.vector.tensor_tensor(onehot_b[:, s % 2], places, rel, ALU.is_equal).then_inc(onehot_done, 1)

            def window_of(i, u, k):
                _, s, n = group(i, u, k)
                return dve.value_load(base_i[0:1, ds(n, 1)], min_val=0, max_val=N - 1)

            def add_window(i, u, k, node):
                _, s, n = group(i, u, k)
                dve.wait_ge(agg_ready, n + 1)
                if not early(n, 1):
                    dve.wait_ge(agg_added, n)
                nodes, heads = acc[:, ds(node, WIN)], z_sum[:, ds(node, WIN)]
                nc.vector.tensor_tensor(nodes, nodes, agg_ps[:, 0:WIN], ALU.add)
                nc.vector.tensor_tensor(heads, heads, agg_ps[0:HEADS, WIN:2 * WIN], ALU.add).then_inc(agg_added, 1)

            def weigh(s, done):
                v = kv[:, s, :, D:KV].rearrange("p j (h d) -> p j h d", d=DH)
                wide = score[:, :].rearrange("p (j h) -> p j h", j=TILES).unsqueeze(3).to_broadcast([P, TILES, HEADS, DH])
                nc.vector.tensor_tensor(v, v, wide, ALU.mult).then_inc(done, 1)

            def edge_turn(i):
                for u in range(UNROLL):
                    t, s, n = group(i, u)
                    b = s % 2
                    left = NG - 1 - n if isinstance(n, int) else UNROLL
                    dve.wait_ge(kv_landed[s], 16 * TILES * (t + 1))
                    dve.wait_ge(qe_ready, n + 1)
                    qe = qe_ps[b][:, :].rearrange("p (j d) -> p j d", j=TILES)
                    nc.vector.tensor_tensor(kq[:, :, :], kv[:, s, :, 0:D], qe, ALU.mult).then_inc(kq_done, 1)
                    if not early(n, 1):
                        node = window_of(i, u, -1)
                    dve.wait_ge(eh_ready, n + 1)
                    dve.wait_ge(kq_done, n + 1)
                    eh = eh_ps[b][:, :].rearrange("p (j d) -> p j d", j=TILES)
                    nc.vector.tensor_tensor(kq[:, :, :], kq[:, :, :], eh, ALU.mult).then_inc(prod_done, 1)
                    dve.wait_ge(prod_done, n + 1)
                    by_head = kq[:, :, :].rearrange("p j (h d) -> p (j h) d", d=DH)
                    nc.vector.tensor_reduce(ssum[:, :], by_head, AX.X, ALU.add).then_inc(ssum_done, 1)
                    dve.wait_ge(ssum_done, n + 1)
                    nc.vector.tensor_scalar(sclip[:, b, :], ssum[:, :], -5.0, 5.0, ALU.max, ALU.min).then_inc(clip_done, 1)
                    if not early(n, 1):
                        add_window(i, u, -1, node)
                    if left >= 3:
                        one_hot(i, u, 3)
                    dve.wait_ge(exp_done, n + 1)
                    weigh(s, msg_done)

            dve.wait_ge(tab_copied, 2 * RT)
            for u in range(2):
                one_hot(0, u, 0)
            dve.wait_ge(inside_sum, 1)
            nc.vector.tensor_reduce(inside_all[:, :], agg_ps[0:1, 0:RT], AX.X, ALU.add).then_inc(stray_step, 1)
            dve.wait_ge(stray_step, 1)
            nc.vector.tensor_scalar(stray_i[:, :], inside_all[:, :], -1.0, float(E), ALU.mult, ALU.add).then_inc(stray_known, 1)
            nc.vector.memset(acc[:, 0:LATE], 0.0).then_inc(msg_clear, 1)
            dve.wait_ge(sco_clear, CHUNKS // 2)
            dve.wait_ge(msg_clear, CHUNKS - EARLY + 1)
            dve.wait_ge(base_landed, 32)
            one_hot(0, 2, 0)
            edge_turn(0)
            with dve.Fori(1, TURNS - 1) as i:
                edge_turn(i)
            edge_turn(TURNS - 1)
            add_window(TURNS - 1, UNROLL - 1, 0, window_of(TURNS - 1, UNROLL - 1, 0))

            def stray_sums(g, last):
                STEPS = 8
                done = g * STEPS
                dve.wait_ge(st_gathered, 16 * 2 * TILES * (g + 1))
                dve.wait_ge(st_products, g + 1)
                nc.vector.tensor_tensor(kq[:, :, :], kv[:, 0, :, 0:D], qe_ps[0][:, :].rearrange("p (j d) -> p j d", j=TILES), ALU.mult).then_inc(st_step, 1)
                dve.wait_ge(st_step, done + 1)
                nc.vector.tensor_tensor(kq[:, :, :], kq[:, :, :], eh_ps[0][:, :].rearrange("p (j d) -> p j d", j=TILES), ALU.mult).then_inc(st_step, 1)
                dve.wait_ge(st_step, done + 2)
                nc.vector.tensor_reduce(ssum[:, :], kq[:, :, :].rearrange("p j (h d) -> p (j h) d", d=DH), AX.X, ALU.add).then_inc(st_step, 1)
                dve.wait_ge(st_step, done + 3)
                nc.vector.tensor_scalar(sclip[:, 1, :], ssum[:, :], -5.0, 5.0, ALU.max, ALU.min).then_inc(st_clip, 1)
                rel = rel_t[:, ds(g, 1), :].rearrange("p a j -> p (a j)")
                nc.vector.tensor_scalar(st_low, rel, 0.0, None, ALU.is_ge).then_inc(st_step, 1)
                dve.wait_ge(st_step, done + 4)
                nc.vector.scalar_tensor_tensor(out=st_in, in0=rel, scalar=float(WIN), in1=st_low, op0=ALU.is_lt, op1=ALU.mult).then_inc(st_step, 1)
                nc.vector.tensor_scalar(st_key_hi, st_ends[:, 1, :], 1.0, None, ALU.add).then_inc(st_step, 1)
                dve.wait_ge(st_step, done + 6)
                nc.vector.tensor_scalar(st_low, st_in, -1.0, 1.0, ALU.mult, ALU.add).then_inc(st_step, 1)
                dve.wait_ge(st_step, done + 7)
                nc.vector.tensor_tensor(st_in, st_key_hi, st_low, ALU.mult).then_inc(st_step, 1)
                dve.wait_ge(st_step, done + 8)
                if last:
                    nc.vector.memset(st_in[0:OLD // TILES, :], 0.0).then_inc(st_step, 1)
                    dve.wait_ge(st_step, done + 9)
                KEYS = 2 * (SWEEP + 1)
                nc.vector.tensor_scalar(st_key, st_in, -1.0, None, ALU.add).then_inc(st_keyed, 1)
                nc.vector.tensor_scalar(st_key_hi, st_in, -1.0 - HALF, None, ALU.add).then_inc(st_keyed, 1)
                dve.wait_ge(st_exp, g + 1)
                weigh(0, st_keyed)

                def sweep(v):
                    n = g * SWEEP + v
                    dve.wait_ge(st_keyed, g * (KEYS + 1) + 2 * v + 3)
                    places = iota[:, 0:HALF].unsqueeze(1).to_broadcast([P, TILES, HALF])
                    for half, key in enumerate((st_key, st_key_hi)):
                        op = nc.vector.tensor_tensor(st_onehot[:, :, half * HALF:(half + 1) * HALF], places,
                                                     key.unsqueeze(2).to_broadcast([P, TILES, HALF]), ALU.is_equal)
                    op.then_inc(st_onehots, 1)
                    dve.wait_ge(st_summed, n + 1)
                    for sums, part in ((acc, st_agg_ps[0]), (z_sum, st_agg_ps[1][0:HEADS])):
                        nodes = sums[:, ds(v * 2 * HALF, 2 * HALF)]
                        op = nc.vector.tensor_tensor(nodes, nodes, part[:, 0:2 * HALF], ALU.add)
                    op.then_inc(st_added, 1)
                    dve.wait_ge(st_added, n + 1)
                    for key in (st_key, st_key_hi):
                        nc.vector.tensor_scalar(key, key, -2.0 * HALF, None, ALU.add).then_inc(st_keyed, 1)

                with dve.Fori(0, SWEEP) as v:
                    sweep(v)
                dve.wait_ge(st_keyed, (g + 1) * (KEYS + 1))
                dve.sem_inc(st_begun, 1)

            dve.wait_ge(agg_added, NG)
            dve.sem_inc(st_begun, 1)
            strays(dve, stray_sums)

            def z_reciprocal(k, b):
                dve.wait_ge(z_turned, k + 1)
                if not early(k, 2):
                    dve.wait_ge(zw_done, k - 1)
                nc.vector.reciprocal(z_rec[0:HQ, b, :], zT_ps[b][0:HQ, 0:TILES * HEADS]).then_inc(zr_done, 1)

            def attend(k, b, n0):
                dve.wait_ge(rT_turned, k + 1)
                m = acc[:, ds(n0, HC)]
                nc.vector.tensor_tensor(m, m, rT_ps[b][:, 0:HC], ALU.mult).then_inc(att_done, 1)

            def measure(k, n0):
                dve.wait_ge(h_done, k + 1)
                nc.vector.bn_stats(hstat[:, ds(k, 1), :].rearrange("p a s -> p (a s)"), acc[:, ds(n0, HC)]).then_inc(hstat_done, 1)

            def attend_step(k, b):
                if not (isinstance(k, int) and k >= HN):
                    z_reciprocal(k, b)
                if not early(k, 2) and not (isinstance(k, int) and k - 2 >= HN):
                    attend(k - 2, b, (k - 2) * HC)
                if not early(k, 4):
                    measure(k - 4, (k - 4) * HC)

            for k in range(4):
                attend_step(k, k % 2)
            with dve.Fori(2, HN // 2) as i:
                for b in range(2):
                    attend_step(i * 2 + b, b)
            for k in range(HN - 1, HN + 4):
                attend_step(k, k % 2)
            dve.wait_ge(hstat_done, HN)
            nc.vector.bn_aggr(bn[:, 0:2], hstat[:, :, :].rearrange("p k s -> p (k s)")).then_inc(bn_step, 1)
            dve.wait_ge(bn_std, 1)
            nc.vector.reciprocal(bn[:, 3:4], bn[:, 2:3]).then_inc(bn_step, 1)
            dve.wait_ge(bn_step, 2)
            nc.vector.tensor_tensor(bn[:, 4:5], bn[:, 3:4], gam[:, :], ALU.mult).then_inc(bn_step, 1)
            dve.wait_ge(bn_step, 3)
            nc.vector.tensor_tensor(bn[:, 5:6], bn[:, 0:1], bn[:, 4:5], ALU.mult).then_inc(bn_step, 1)
            dve.wait_ge(bn_step, 4)
            nc.vector.tensor_tensor(bn[:, 6:7], bet[:, :], bn[:, 5:6], ALU.subtract).then_inc(bn_step, 1)
            dve.wait_ge(bn_step, 5)

            def norm_nodes(c, b, n0, parts=P):
                if not early(c, 2):
                    dve.wait_ge(y_done, c - 1)
                nodes = parts * TILES
                nc.vector.tensor_scalar(eaT[:, b, 0:nodes], acc[:, ds(n0, nodes)], bn[:, 4:5], bn[:, 6:7], ALU.mult, ALU.add).then_inc(y1_done, 1)

            def y_stats(c, s, parts=P):
                dve.wait_ge(yT_ready, c + 1)
                for j in range(TILES):
                    last = nc.vector.bn_stats(ystat[0:parts, s, j, :], yT_ps[s][0:parts, j * P:(j + 1) * P])
                last.then_inc(ystat_done, 1)

            def y_aggregate(c, s, parts=P):
                dve.wait_ge(ystat_done, c + 1)
                dve.sem_inc(aggr_begun, 1)
                for j in range(TILES):
                    last = nc.vector.bn_aggr(ymv[0:parts, s, j, :], ystat[0:parts, s, j, :])
                last.then_inc(yaggr_done, 1)

            def y_reciprocal(c, s, parts=P):
                dve.wait_ge(ystd_done, c + 1)
                nc.vector.reciprocal(yrec[0:parts, s, :], ystd[0:parts, s, :]).then_inc(yrec_done, 1)

            def y_shift(c, s, parts=P):
                dve.wait_ge(yrec_done, c + 1)
                nc.vector.scalar_tensor_tensor(out=ymr[0:parts, s, :], in0=ymv[0:parts, s, :, 0:1].rearrange("p j a -> p (j a)"), scalar=-1.0,
                                               in1=yrec[0:parts, s, :], op0=ALU.mult, op1=ALU.mult).then_inc(ynorm_known, 1)

            def norm_step(i, u, ahead=P, parts=P):
                _, s, c = group(i, u)
                _, s1, c1 = group(i, u, -1)
                y_stats(c, s, parts)
                if not early(c, 1):
                    y_reciprocal(c1, s1)
                if ahead:
                    norm_nodes(c + 3, (s + 1) % 2, (c + 3) * NB, ahead)
                y_aggregate(c, s, parts)
                if not early(c, 1):
                    y_shift(c1, s1)

            for c in range(3):
                norm_nodes(c, c % 2, c * NB)
            for u in range(UNROLL):
                norm_step(0, u)
            with dve.Fori(1, NTURNS - 1) as i:
                for u in range(UNROLL):
                    norm_step(i, u)
            for u in range(UNROLL):
                norm_step(NTURNS - 1, u, ahead=(P, PLAST, 0, 0)[u])
            norm_step(NTURNS, 0, ahead=0, parts=PLAST)
            y_reciprocal(CHUNKS, 0, PLAST)
            y_shift(CHUNKS, 0, PLAST)


_INS = ["x", "src", "dst", "edge_attr_128", "L0_gnn_WQ", "L0_gnn_WK", "L0_gnn_WV", "L0_gnn_WE", "L0_gnn_bn_gamma", "L0_gnn_bn_beta"]


def kernel(**inputs):
    import numpy as np
    import concourse.bacc as bacc
    from concourse import mybir
    from concourse.bass_utils import run_bass_kernel_spmd

    nc = bacc.Bacc("TRN2", target_bir_lowering=False, num_devices=1)
    arrays, args = {}, []
    for name in _INS:
        a = np.ascontiguousarray(inputs[name])
        arrays[f"in_{name}"] = a
        args.append(nc.dram_tensor(f"in_{name}", a.shape, mybir.dt.from_np(a.dtype), kind="ExternalInput").ap())
    x = arrays["in_x"]
    args.append(nc.dram_tensor("out", x.shape, mybir.dt.from_np(x.dtype), kind="ExternalOutput").ap())
    build(nc, *args)
    result = run_bass_kernel_spmd(nc, [arrays], core_ids=[0])
    return result.results[0]["out"]
```
